# Optimizing a Trainium2 kernel written in Bass

```python
import numpy as np
import jax
import jax.numpy as jnp

def _softmax(x, axis=-1):
    return jax.nn.softmax(x, axis=axis)

def _gelu(x):
    return jax.nn.gelu(x, approximate=True)

def _silu(x):
    return jax.nn.silu(x)

def _sigmoid(x):
    return jax.nn.sigmoid(x)

def _layernorm(x, axis=-1, eps=1e-05):
    m = jnp.mean(x, axis=axis, keepdims=True)
    v = jnp.var(x, axis=axis, keepdims=True)
    return (x - m) / jnp.sqrt(v + eps)

def _scatter_add(tgt, idx, src, axis=0):
    return tgt.at[idx].add(src)

def _segment_sum(src, seg, n):
    return jax.ops.segment_sum(src, seg, n)
kernel_name = 'mk_xattn_ffn_d1_seqx_r4_04f980'

def setup_inputs(seed: int=0):
    np.random.seed(seed)
    _w = jnp.asarray

    def _rec_inputs():
        import jax
        import jax.numpy as jnp
        _rk = jax.random.key(seed)
        x = -0.000125 + 0.9999 * jax.random.normal(jax.random.fold_in(_rk, 1), (4, 512, 512), jnp.float32)
        _lenS = 512 - jax.random.randint(jax.random.fold_in(_rk, 7), (4,), 0, max(1, 512 // 4) + 1, jnp.int32)
        _lenS2 = 512 - jax.random.randint(jax.random.fold_in(_rk, 8), (4,), 0, max(1, 512 // 4) + 1, jnp.int32)
        itok_BxS_13_99985 = jax.random.randint(jax.random.fold_in(_rk, 11), (4, 512), 13, 99986, jnp.int32)
        _ctx_2048P = jax.random.normal(jax.random.fold_in(_rk, 12), (4, 16, 512), jnp.float32)
        _ctx_2048c = jax.random.dirichlet(jax.random.fold_in(_rk, 512), 0.3 * jnp.ones((16,), jnp.float32), (4, 512))
        _ctx_2048t = jnp.einsum('bsk,bkd->bsd', _ctx_2048c, _ctx_2048P)
        _ctx_2048t = _ctx_2048t * jax.lax.rsqrt(jnp.mean(jnp.square(_ctx_2048t)) + 1e-12) * 0.953939
        ctx_2048 = 6.82029e-06 + 0.0200006 * (_ctx_2048t + 0.3 * jax.random.normal(jax.random.fold_in(_rk, 612), (4, 512, 512), jnp.float32))
        return (x, itok_BxS_13_99985, ctx_2048)
    x, itok_BxS_13_99985, ctx_2048 = _rec_inputs()

    def _L0_xattn_setup():
        import jax, jax.numpy as jnp
        import numpy as np
        B, S, D = (4, 1024, 512)
        E = 4
        F = 2048 // E
        VOCAB = 25000
        key = jax.random.key(seed)
        k1, k2, k3, k4, k5 = jax.random.split(key, 5)
        hidden_states = jax.random.normal(k1, (B, S, D), dtype=jnp.float32)
        token_ids = jax.random.randint(k2, (B, S), 0, VOCAB, dtype=jnp.int64)
        Wg = jax.random.normal(k3, (E, F, D), dtype=jnp.float32) * 0.02
        Wu = jax.random.normal(k4, (E, F, D), dtype=jnp.float32) * 0.02
        Wd = jax.random.normal(k5, (E, D, F), dtype=jnp.float32) * 0.02
        return {'hidden_states': hidden_states, 'token_ids': token_ids, 'Wg': Wg, 'Wu': Wu, 'Wd': Wd}
    _L0_xattn_all = _L0_xattn_setup()
    _L0_xattn_in = {k: v for k, v in _L0_xattn_all.items() if k in ()}
    del _L0_xattn_all

    def _L0_ffn_setup():
        import jax, jax.numpy as jnp
        import numpy as np

        def binarize_weight(w):
            alpha = jnp.mean(jnp.abs(w), axis=tuple(range(1, w.ndim)), keepdims=True)
            bw = jnp.where(w >= 0, 1.0, -1.0) * alpha
            return jax.lax.stop_gradient(bw - w) + w
        key = jax.random.key(seed)
        k1, k2, k3 = jax.random.split(key, 3)
        in_features, out_features = (512, 512)
        x = jax.random.normal(k1, (8, 512, in_features), dtype=jnp.float32)
        std = np.sqrt(2.0 / out_features).astype(np.float32)
        weight = jax.random.normal(k2, (out_features, in_features), dtype=jnp.float32) * std
        bias = jax.random.normal(k3, (out_features,), dtype=jnp.float32) * 0.01
        return {'x': x, 'weight': weight, 'bias': bias}
    _L0_ffn_all = _L0_ffn_setup()
    _L0_ffn_in = {k: v for k, v in _L0_ffn_all.items() if k in ('weight', 'bias')}
    del _L0_ffn_all
    return {'x': x, 'itok_BxS_13_99985': itok_BxS_13_99985, 'ctx_2048': ctx_2048, 'L0_ffn_weight': _L0_ffn_in['weight'], 'L0_ffn_bias': _L0_ffn_in['bias']}

def reference(x, itok_BxS_13_99985, ctx_2048, L0_ffn_weight, L0_ffn_bias):
    import jax
    import jax.numpy as jnp

    def _L0_xattn_ref(hidden_states, token_ids, Wg, Wu, Wd):
        import jax, jax.numpy as jnp
        import numpy as np
        B, S, D = (4, 1024, 512)
        E = 4
        F = 2048 // E
        VOCAB = 25000
        tokens_per_expert = VOCAB // E
        tid = jnp.clip(token_ids, 0, VOCAB - 1)
        expert_ids = jnp.minimum(tid // tokens_per_expert, E - 1)
        out = jnp.zeros_like(hidden_states)
        for e in range(E):
            g = jax.nn.silu(jnp.einsum('bsd,fd->bsf', hidden_states, Wg[e]))
            u = jnp.einsum('bsd,fd->bsf', hidden_states, Wu[e])
            y = jnp.einsum('bsf,df->bsd', g * u, Wd[e])
            out = jnp.where((expert_ids == e)[..., None], y, out)
        return out

    def _L0_ffn_ref(x, weight, bias):
        import jax, jax.numpy as jnp
        import numpy as np

        def binarize_weight(w):
            alpha = jnp.mean(jnp.abs(w), axis=tuple(range(1, w.ndim)), keepdims=True)
            bw = jnp.where(w >= 0, 1.0, -1.0) * alpha
            return jax.lax.stop_gradient(bw - w) + w
        bw = binarize_weight(weight)
        return jnp.einsum('bsi,oi->bso', x, bw) + bias
    x = x + _L0_xattn_ref(_layernorm(x, axis=-1), itok_BxS_13_99985, ctx_2048, ctx_2048, ctx_2048)
    x = x + _L0_ffn_ref(_layernorm(x, axis=-1), L0_ffn_weight, L0_ffn_bias)
    return x

_drawn_inputs = setup_inputs


def setup_inputs(seed=0):
    import zlib

    import numpy as np

    out = dict(_drawn_inputs(seed))
    spreads = {}
    factors = {'L0_ffn_bias': 8.0}
    for name, (base, spread) in spreads.items():
        noise = np.random.default_rng([zlib.crc32(name.encode()), seed]).standard_normal(out[name].shape)
        drawn = base * np.exp(spread * noise) if base else spread * noise
        out[name] = jnp.asarray(drawn.astype(out[name].dtype))
    for name, factor in factors.items():
        out[name] = (out[name] * factor).astype(out[name].dtype)
    return out
```

```python
from contextlib import ExitStack

import concourse.bass as bass
from concourse import mybir

P = 128
D = 512
KD = D // P
E = 4
VOCAB = 25000
PER_EXPERT = VOCAB // E
T = 4 * 512
NC = T // P
NT = NC + E - 1
NTP = NT + 1
EPS = 1e-5

LOOP_FROM, LOOP_TO = 4, NT - 3
LAST = NT + 2


def xattn_ffn(nc, x, token_ids, ctx_w, weight, bias, out):
    f32, f32r, f16, i32 = mybir.dt.float32, mybir.dt.float32r, mybir.dt.float16, mybir.dt.int32
    ALU, ACT, AX = mybir.AluOpType, mybir.ActivationFunctionType, mybir.AxisListType

    ctx = ExitStack()
    with ctx:
        def sb(name, shape, dt=f32):
            return ctx.enter_context(nc.sbuf_tensor(name, shape, dt))

        def sem(name):
            return ctx.enter_context(nc.semaphore(name))

        def bank(name):
            return ctx.enter_context(nc.psum_tensor(name, [P, D], f32))

        ps_hT, ps_z, ps_gT, ps_y = bank("ps_hT"), bank("ps_z"), bank("ps_gT"), bank("ps_y")
        ps_h2T, ps_m = bank("ps_h2T"), bank("ps_m")
        ps_prep = [bank("ps_prep0"), bank("ps_prep1")]
        ps_rank, ps_chunk_sum, ps_total, ps_slot = ps_y[:, 0:E * NC], ps_m[:, 0:1], ps_h2T[:, 0:E], ps_gT[:, 0:NTP]

        nat = sb("nat", [P, E + 1, KD, D])
        ct_hi = sb("ct_hi", [P, E * KD * D], f32r)
        ct_lo = sb("ct_lo", [P, E * KD * D], f32r)
        half_sign = sb("half_sign", [P, KD, D], f32r)
        alpha2 = sb("alpha2", [P, D])
        bias_bc = sb("bias_bc", [P, D])
        ident = sb("ident", [P, P])
        ones = sb("ones", [P, P])
        before = sb("before", [P, P], f16)
        ones_col = sb("ones_col", [P, 2], f16)
        chunk_before = sb("chunk_before", [P, E, NC], f16)
        chunk_of = sb("chunk_of", [P, E], f16)
        iota_lane = sb("iota_lane", [P, P], f16)
        iota_tile = sb("iota_tile", [P, NTP])
        iota_128 = sb("iota_128", [P, NC])
        token_no = sb("token_no", [P, NC])
        dropped = sb("dropped", [P, 1])
        minus_half = sb("minus_half", [P, 1])
        tid = sb("tid", [P, NC], i32)
        reached = sb("reached", [P, E + 1, NC])
        onehot = sb("onehot", [P, 2 * E, NC], f16)
        chunk_sum = sb("chunk_sum", [P, P], f16)
        full = sb("full", [P, E, NC])
        tiles_of = sb("tiles_of", [P, E])
        tile_from = sb("tile_from", [P, E])
        rank = sb("rank", [P, E, NC])
        rank1 = sb("rank1", [P, E, NC])
        slot = sb("slot", [P, NC], i32)
        lane_i, tile_i = sb("lane_i", [P, NC], i32), sb("tile_i", [P, NC], i32)
        lane, tile = sb("lane", [P, NC]), sb("tile", [P, NC])
        lane_hot = sb("lane_hot", [P, NC, P], f16)
        tile_hot = sb("tile_hot", [P, NC, NTP])
        tile_val = sb("tile_val", [P, NC, NTP], f16)
        is_empty = sb("is_empty", [P, NTP])
        gather_idx = sb("gather_idx", [P, NTP], i32)
        scatter_idx = sb("scatter_idx", [P, NTP], i32)
        at_least_e = sb("at_least_e", [P, E - 1, NTP])
        expert_of = sb("expert_of", [P, NTP], i32)
        xs = sb("xs", [P, NT * D])
        bn1, bn2 = sb("bn1", [P, 6]), sb("bn2", [P, 6])
        mv1, mv2 = sb("mv1", [P, 2]), sb("mv2", [P, 2])
        var1, var2 = sb("var1", [P, 1]), sb("var2", [P, 1])
        rs1, rs2 = sb("rs1", [P, 1]), sb("rs2", [P, 1])
        nm1, nm2 = sb("nm1", [P, 1]), sb("nm2", [P, 1])
        h, h2 = sb("h", [P, D]), sb("h2", [P, D])
        hT_hi, hT_lo = sb("hT_hi", [P, D], f32r), sb("hT_lo", [P, D], f32r)
        silu, gu = sb("silu", [P, D]), sb("gu", [P, D])
        gT_hi, gT_lo = sb("gT_hi", [P, D], f32r), sb("gT_lo", [P, D], f32r)
        h2T_hi, h2T_lo = sb("h2T_hi", [P, D], f32r), sb("h2T_lo", [P, D], f32r)
        scaled = sb("scaled", [P, D])
        row_abs = sb("row_abs", [P, KD])
        abs_bc = sb("abs_bc", [P, KD, P])
        out_rows = [sb("out_rows0", [P, D]), sb("out_rows1", [P, D])]
        out_idx = [sb("out_idx0", [P, 1], i32), sb("out_idx1", [P, 1], i32)]

        s_stats1, s_const1, s_h = sem("s_stats1"), sem("s_const1"), sem("s_h")
        s_hT_ps, s_hT_hi, s_hT_lo = sem("s_hT_ps"), sem("s_hT_hi"), sem("s_hT_lo")
        s_z, s_silu, s_gu = sem("s_z"), sem("s_silu"), sem("s_gu")
        s_gT_ps, s_gT_hi, s_gT_lo = sem("s_gT_ps"), sem("s_gT_hi"), sem("s_gT_lo")
        s_y, s_x1, s_stats2, s_const2, s_h2 = sem("s_y"), sem("s_x1"), sem("s_stats2"), sem("s_const2"), sem("s_h2")
        s_h2T_ps, s_h2T_hi, s_h2T_lo = sem("s_h2T_ps"), sem("s_h2T_hi"), sem("s_h2T_lo")
        s_m, s_scaled, s_xb, s_out = sem("s_m"), sem("s_scaled"), sem("s_xb"), sem("s_out")
        s_bn1, s_bn2 = sem("s_bn1"), sem("s_bn2")
        s_var1, s_rs1 = sem("s_var1"), sem("s_rs1")
        s_var2, s_rs2 = sem("s_var2"), sem("s_rs2")
        s_out_idx = sem("s_out_idx")
        s_scattered = [sem("s_scattered0"), sem("s_scattered1")]
        EARLY = LOOP_FROM + 3
        s_x = [sem(f"s_rows{j}") for j in range(EARLY)]
        s_x_rest = sem("s_rows_rest")
        s_tid, s_bias = sem("s_tid"), sem("s_bias")
        s_nat = [sem(f"s_nat{w}") for w in range(E + 1)]
        s_ident, s_mask0, s_masks, s_iotas = sem("s_ident"), sem("s_mask0"), sem("s_masks"), sem("s_iotas")
        s_prep_ps, s_prep_hi, s_prep_lo = sem("s_prep_ps"), sem("s_prep_hi"), sem("s_prep_lo")
        s_row_abs, s_abs_bc, s_alpha_ps, s_alpha = sem("s_row_abs"), sem("s_abs_bc"), sem("s_alpha_ps"), sem("s_alpha")
        s_waited = sem("s_waited")
        s_route = sem("s_route")
        s_onehot_ps, s_rank_ps, s_slot_ps = sem("s_onehot_ps"), sem("s_rank_ps"), sem("s_slot_ps")
        s_gather_idx, s_scatter_idx, s_expert = sem("s_gather_idx"), sem("s_scatter_idx"), sem("s_expert")

        R = {name: n + 1 for n, name in enumerate((
            "zeroed", "reached0", "reached_end", "reached1", "reached2", "reached3", "onehot", "chunk_sum",
            "full", "tiles0", "tiles_of", "from0", "from1", "from2", "from3", "shifted", "masked", "slot",
            "lane_i", "tile_i", "lane", "tile", "lane_hot", "tile_hot", "tile_val", "empty", "at_least"))}

        WEIGHT = E
        PREPS = {-1: [0], 0: [1, WEIGHT], 1: [2], 2: [3]}
        prep_order = [(w, k) for i in (-1, 0, 1, 2) for w in PREPS[i] for k in range(KD)]
        prep_no = {wk: n for n, wk in enumerate(prep_order)}

        def tile_of(buf, j):
            return buf[:, bass.ds(j * D, D)]

        def has(j):
            return not isinstance(j, int) or 0 <= j < NT

        def at_least(eng, s, n):
            if not isinstance(n, int) or n > 0:
                eng.wait_ge(s, n)

        def waited(eng):
            eng.sem_inc(s_waited, 1)

        def iterate(eng, body):
            for i in range(0, LOOP_FROM):
                body(i)
            with eng.Fori(LOOP_FROM, LOOP_TO) as i:
                body(i)
            for i in range(LOOP_TO, LAST + 1):
                body(i)

        block = ctx.enter_context(nc.Block())

        @block.sync
        def _(sp):
            sp.dma_start(tid[:], token_ids.rearrange("(p c) -> p c", p=P)).then_inc(s_tid, 16)
            for w in (0, 1, WEIGHT, 2, 3):
                src = weight if w == WEIGHT else ctx_w[w]
                sp.dma_start(nat[:, w], src.rearrange("(b p) d -> p b d", p=P)).then_inc(s_nat[w], 16)
            sp.dma_start(bias_bc[:], bias.partition_broadcast(P)).then_inc(s_bias, 16)

        @block.gpsimd
        def _(pool):
            g = nc.gpsimd
            g.memset(ident[:], 0.0).then_inc(s_mask0, 1)
            g.memset(before[:], 1.0).then_inc(s_mask0, 1)
            g.memset(chunk_before[:], 1.0).then_inc(s_mask0, 1)
            g.memset(chunk_of[:], 1.0).then_inc(s_mask0, 1)
            g.memset(ones_col[:], 1.0).then_inc(s_masks, 1)
            g.memset(minus_half[:], -0.5).then_inc(s_masks, 1)
            pool.wait_ge(s_mask0, 4)
            g.affine_select(out=before[:], in_=before[:], compare_op=ALU.is_gt, fill=0.0, base=0,
                            pattern=[[1, P]], channel_multiplier=-1).then_inc(s_masks, 1)
            g.affine_select(out=chunk_before[:], in_=chunk_before[:], compare_op=ALU.is_gt, fill=0.0, base=0,
                            pattern=[[NC, E], [1, NC]], channel_multiplier=-1).then_inc(s_mask0, 1)
            g.affine_select(out=chunk_of[:], in_=chunk_of[:], compare_op=ALU.is_ge, fill=0.0, base=0,
                            pattern=[[-NC, E]], channel_multiplier=1).then_inc(s_mask0, 1)
            g.affine_select(out=ident[:], in_=ident[:], compare_op=ALU.not_equal, fill=1.0, base=0,
                            pattern=[[-1, P]], channel_multiplier=1).then_inc(s_ident, 1)
            pool.wait_ge(s_mask0, 6)
            g.affine_select(out=chunk_before[:], in_=chunk_before[:], compare_op=ALU.is_ge, fill=0.0, base=0,
                            pattern=[[-NC, E], [0, NC]], channel_multiplier=1).then_inc(s_masks, 1)
            g.affine_select(out=chunk_of[:], in_=chunk_of[:], compare_op=ALU.is_ge, fill=0.0, base=NC - 1,
                            pattern=[[NC, E]], channel_multiplier=-1).then_inc(s_masks, 1)
            g.iota(iota_128[:], pattern=[[P, NC]], base=0, channel_multiplier=0,
                   allow_small_or_imprecise_dtypes=True).then_inc(s_iotas, 1)
            g.iota(iota_lane[:], pattern=[[1, P]], base=0, channel_multiplier=0,
                   allow_small_or_imprecise_dtypes=True).then_inc(s_iotas, 1)
            g.iota(iota_tile[:], pattern=[[1, NTP]], base=0, channel_multiplier=0,
                   allow_small_or_imprecise_dtypes=True).then_inc(s_iotas, 1)
            g.iota(token_no[:], pattern=[[1, NC]], base=1, channel_multiplier=NC,
                   allow_small_or_imprecise_dtypes=True).then_inc(s_iotas, 1)
            g.iota(dropped[:], pattern=[[1, 1]], base=1 + T, channel_multiplier=1,
                   allow_small_or_imprecise_dtypes=True).then_inc(s_iotas, 1)

            def gather(j):
                pool.indirect_dma_start(
                    out=xs[:, j * D:(j + 1) * D], out_offset=None, in_=x,
                    in_offset=bass.IndirectOffsetOnAxis(ap=gather_idx[:, j:j + 1], axis=0),
                    bounds_check=T - 1, oob_is_err=False).then_inc(s_x[j] if j < EARLY else s_x_rest, 16)

            def constants(j, mv, var, rs, nm, s_stats, s_var, s_rs, s_done, s_used):
                at_least(pool, s_stats, j + 1)
                waited(pool)
                g.tensor_scalar(var[:], mv[:, 1:2], EPS, None, ALU.add).then_inc(s_var, 1)
                pool.wait_ge(s_var, j + 1)
                at_least(pool, s_used, j)
                g.tensor_tensor(rs[:], var[:], minus_half[:], ALU.pow).then_inc(s_rs, 1)
                pool.wait_ge(s_rs, j + 1)
                waited(pool)
                g.tensor_scalar(nm[:], mv[:, 0:1], rs[:], -1.0, ALU.mult, ALU.mult).then_inc(s_done, 1)

            def constants1(j):
                constants(j, mv1, var1, rs1, nm1, s_stats1, s_var1, s_rs1, s_const1, s_h)

            def finish(j, half):
                at_least(pool, s_scaled, j + 1)
                at_least(pool, s_xb, j + 1)
                if not isinstance(j, int) or j >= 2:
                    pool.wait_ge(s_scattered[half], (j - half) * 8)
                g.tensor_tensor(out_rows[half][:], tile_of(xs, j), scaled[:], ALU.add).then_inc(s_out, 1)
                g.tensor_copy(out_idx[half][:], scatter_idx[:, bass.ds(j, 1)]).then_inc(s_out_idx, 1)
                pool.wait_ge(s_out, j + 1)
                pool.wait_ge(s_out_idx, j + 1)
                waited(pool)
                pool.indirect_dma_start(
                    out=out, out_offset=bass.IndirectOffsetOnAxis(ap=out_idx[half][:], axis=0),
                    in_=out_rows[half][:], in_offset=None,
                    bounds_check=T - 1, oob_is_err=False).then_inc(s_scattered[half], 16)

            pool.wait_ge(s_gather_idx, 1)
            for j in range(4):
                gather(j)
            constants1(0)
            gather(4)
            constants1(1)
            gather(5)
            pool.wait_ge(s_bias, 16)

            def body(i, half):
                if has(i - 3):
                    if isinstance(i, int) and i == 3:
                        pool.wait_ge(s_scatter_idx, 1)
                    finish(i - 3, 1 - half)
                if has(i + 2):
                    constants1(i + 2)
                if isinstance(i, int) and i < LOOP_FROM:
                    for j in range(6 + i * 4, min(NT, 10 + i * 4)):
                        gather(j)
                if has(i - 1):
                    constants(i - 1, mv2, var2, rs2, nm2, s_stats2, s_var2, s_rs2, s_const2, s_h2)
                    at_least(pool, s_h2, i)
                    g.tensor_tensor(tile_of(xs, i - 1), tile_of(xs, i - 1), bias_bc[:], ALU.add).then_inc(s_xb, 1)

            for i in range(0, LOOP_FROM):
                body(i, i % 2)
            with pool.Fori(LOOP_FROM, LOOP_TO, 2) as i:
                body(i, 0)
                body(i + 1, 1)
            for i in range(LOOP_TO, LAST + 1):
                body(i, i % 2)
            pool.wait_ge(s_scattered[0], 16 * ((NT + 1) // 2))
            pool.wait_ge(s_scattered[1], 16 * (NT // 2))

        @block.scalar
        def _(act):
            a = nc.scalar

            def prep_hi(w):
                if w == WEIGHT:
                    return
                for k in range(KD):
                    n = prep_no[w, k]
                    act.wait_ge(s_prep_ps, n + 1)
                    at = (w * KD + k) * D
                    a.activation(ct_hi[:, at:at + D], ps_prep[n % 2][:], ACT.Copy).then_inc(s_prep_hi, 1)

            def norm1(j):
                at_least(act, s_const1, j + 1)
                at_least(act, s_hT_ps, j)
                a.activation(h[:], tile_of(xs, j), ACT.Identity, bias=nm1[:], scale=rs1[:]).then_inc(s_h, 1)

            def body(i):
                if has(i):
                    at_least(act, s_z, i + 1)
                    a.activation(silu[:], ps_z[:], ACT.Silu).then_inc(s_silu, 1)
                if has(i - 2):
                    at_least(act, s_h2T_ps, i - 1)
                    at_least(act, s_m, i - 2)
                    a.activation(h2T_hi[:], ps_h2T[:], ACT.Copy).then_inc(s_h2T_hi, 1)
                if has(i + 1):
                    at_least(act, s_hT_ps, i + 2)
                    a.activation(hT_hi[:], ps_hT[:], ACT.Copy).then_inc(s_hT_hi, 1)
                if isinstance(i, int) and i in PREPS:
                    for w in PREPS[i]:
                        prep_hi(w)
                if has(i + 2):
                    norm1(i + 2)
                if has(i):
                    at_least(act, s_gT_ps, i + 1)
                    a.activation(gT_hi[:], ps_gT[:], ACT.Copy).then_inc(s_gT_hi, 1)
                if has(i - 1):
                    at_least(act, s_const2, i)
                    at_least(act, s_h2T_ps, i - 1)
                    a.activation(h2[:], tile_of(xs, i - 1), ACT.Identity, bias=nm2[:], scale=rs2[:]).then_inc(s_h2, 1)
                if isinstance(i, int) and i == 0:
                    act.wait_ge(s_nat[WEIGHT], 16)
                    for b in range(KD):
                        a.activation(silu[:], nat[:, WEIGHT, b], ACT.Abs,
                                     accum_out=row_abs[:, b:b + 1]).then_inc(s_row_abs, 1)
                        act.wait_ge(s_row_abs, b + 1)
                    act.wait_ge(s_alpha_ps, 1)
                    a.activation(alpha2[:], ps_m[:], ACT.Copy).then_inc(s_alpha, 1)

            prep_hi(0)
            norm1(0)
            act.wait_ge(s_hT_ps, 1)
            a.activation(hT_hi[:], ps_hT[:], ACT.Copy).then_inc(s_hT_hi, 1)
            norm1(1)
            iterate(act, body)

        @block.vector
        def _(dve):
            v = nc.vector
            v.memset(ones[:], 1.0).then_inc(s_route, 1)

            def step(name, ins):
                ins.then_inc(s_route, 1)

            def after(name):
                dve.wait_ge(s_route, R[name])

            step("reached0", v.memset(reached[:, 0], 1.0))
            step("reached_end", v.memset(reached[:, E], 0.0))
            dve.wait_ge(s_tid, 16)
            for e in range(1, E):
                step(f"reached{e}", v.tensor_scalar(reached[:, e], tid[:], float(PER_EXPERT * e), None, ALU.is_ge))
            v.memset(onehot[:, E:2 * E], 0.0).then_inc(s_masks, 1)
            after("reached3")
            step("onehot", v.tensor_tensor(onehot[:, 0:E], reached[:, 0:E], reached[:, 1:E + 1], ALU.subtract))
            dve.wait_ge(s_onehot_ps, 1)
            step("chunk_sum", v.tensor_scalar(chunk_sum[:], ones[:], ps_chunk_sum, None, ALU.mult))
            dve.wait_ge(s_iotas, 5)
            dve.wait_ge(s_rank_ps, 1)
            step("full", v.tensor_tensor(full[:], ps_total.unsqueeze(2).broadcast_to([P, E, NC]),
                                         iota_128[:].unsqueeze(1).broadcast_to([P, E, NC]), ALU.is_gt))
            after("full")
            step("tiles0", v.tensor_reduce(tiles_of[:], full[:], AX.X, ALU.add))
            after("tiles0")
            step("tiles_of", v.tensor_scalar(tiles_of[:], tiles_of[:], 1.0, None, ALU.max))
            step("from0", v.memset(tile_from[:, 0:1], 0.0))
            for e in range(1, E):
                after(f"from{e - 1}")
                step(f"from{e}", v.tensor_tensor(tile_from[:, e:e + 1], tile_from[:, e - 1:e],
                                                 tiles_of[:, e - 1:e], ALU.add))
            after("from3")
            step("shifted", v.scalar_tensor_tensor(
                out=rank1[:], in0=tile_from[:].unsqueeze(2).broadcast_to([P, E, NC]), scalar=float(P),
                in1=ps_rank.rearrange("p (e c) -> p e c", e=E), op0=ALU.mult, op1=ALU.add))
            after("shifted")
            step("masked", v.tensor_tensor(rank[:], rank1[:], onehot[:, 0:E], ALU.mult))
            after("masked")
            with nc.allow_low_precision(reason="whole numbers below 2^12"):
                step("slot", v.tensor_reduce(slot[:], rank[:].rearrange("p e c -> p c e"), AX.X, ALU.add))
            after("slot")
            step("lane_i", v.tensor_scalar(lane_i[:], slot[:], P - 1, None, ALU.bitwise_and))
            step("tile_i", v.tensor_scalar(tile_i[:], slot[:], P.bit_length() - 1, None, ALU.logical_shift_right))
            after("tile_i")
            step("lane", v.tensor_copy(lane[:], lane_i[:]))
            step("tile", v.tensor_copy(tile[:], tile_i[:]))
            after("tile")
            for c in range(NC):
                last = v.tensor_scalar(lane_hot[:, c], iota_lane[:], lane[:, c:c + 1], None, ALU.is_equal)
            step("lane_hot", last)
            step("tile_hot", v.tensor_tensor(tile_hot[:], tile[:].unsqueeze(2).broadcast_to([P, NC, NTP]),
                                             iota_tile[:].unsqueeze(1).broadcast_to([P, NC, NTP]), ALU.is_equal))
            after("tile_hot")
            step("tile_val", v.tensor_tensor(tile_val[:], tile_hot[:],
                                             token_no[:].unsqueeze(2).broadcast_to([P, NC, NTP]), ALU.mult))
            dve.wait_ge(s_slot_ps, 1)
            v.tensor_scalar(gather_idx[:], ps_slot, 1.0, 0.0, ALU.subtract, ALU.max).then_inc(s_gather_idx, 1)
            step("empty", v.tensor_scalar(is_empty[:], ps_slot, 0.0, dropped[:], ALU.is_equal, ALU.mult))
            step("at_least", v.tensor_tensor(at_least_e[:], iota_tile[:].unsqueeze(1).broadcast_to([P, E - 1, NTP]),
                                             tile_from[:, 1:E].unsqueeze(2).broadcast_to([P, E - 1, NTP]), ALU.is_ge))
            after("at_least")
            v.scalar_tensor_tensor(out=scatter_idx[:], in0=ps_slot, scalar=-1.0, in1=is_empty[:],
                                   op0=ALU.add, op1=ALU.add).then_inc(s_scatter_idx, 1)
            with nc.allow_low_precision(reason="whole numbers below 4"):
                v.tensor_reduce(expert_of[:], at_least_e[:].rearrange("p e t -> p t e"), AX.X, ALU.add)\
                 .then_inc(s_expert, 1)

            def prep_lo(w):
                for k in range(KD):
                    n = prep_no[w, k]
                    if w == WEIGHT:
                        dve.wait_ge(s_prep_ps, n + 1)
                        v.tensor_scalar(half_sign[:, k], ps_prep[n % 2][:], 0.0, -0.5, ALU.is_ge, ALU.add)\
                         .then_inc(s_prep_lo, 1)
                    else:
                        dve.wait_ge(s_prep_hi, sum(o[0] != WEIGHT for o in prep_order[:n + 1]))
                        at = (w * KD + k) * D
                        v.tensor_tensor(ct_lo[:, at:at + D], ps_prep[n % 2][:], ct_hi[:, at:at + D].bitcast(f32),
                                        ALU.subtract).then_inc(s_prep_lo, 1)

            def stats1(j):
                if isinstance(j, int) and j < EARLY:
                    dve.wait_ge(s_x[j], 16)
                at_least(dve, s_stats1, j)
                waited(dve)
                v.bn_stats(bn1[:], tile_of(xs, j)).then_inc(s_bn1, 1)
                dve.wait_ge(s_bn1, j + 1)
                at_least(dve, s_const1, j)
                waited(dve)
                v.bn_aggr(mv1[:], bn1[:]).then_inc(s_stats1, 1)

            def rest(lo, ps, hi, s_hi, s_lo, j):
                at_least(dve, s_hi, j + 1)
                v.tensor_tensor(lo[:], ps[:], hi[:].bitcast(f32), ALU.subtract).then_inc(s_lo, 1)

            def body(i):
                if has(i - 3):
                    if isinstance(i, int) and i == 3:
                        dve.wait_ge(s_alpha, 1)
                    at_least(dve, s_m, i - 2)
                    at_least(dve, s_out, i - 3)
                    v.tensor_tensor(scaled[:], ps_m[:], alpha2[:], ALU.mult).then_inc(s_scaled, 1)
                if has(i):
                    at_least(dve, s_silu, i + 1)
                    at_least(dve, s_gT_ps, i)
                    v.tensor_tensor(gu[:], ps_z[:], silu[:], ALU.mult).then_inc(s_gu, 1)
                if has(i - 2):
                    rest(h2T_lo, ps_h2T, h2T_hi, s_h2T_hi, s_h2T_lo, i - 2)
                if has(i + 1):
                    rest(hT_lo, ps_hT, hT_hi, s_hT_hi, s_hT_lo, i + 1)
                if isinstance(i, int) and i in PREPS:
                    for w in PREPS[i]:
                        prep_lo(w)
                if has(i + 3):
                    stats1(i + 3)
                if has(i - 1):
                    at_least(dve, s_y, i)
                    v.tensor_tensor(tile_of(xs, i - 1), ps_y[:], tile_of(xs, i - 1), ALU.add).then_inc(s_x1, 1)
                    dve.wait_ge(s_x1, i)
                    at_least(dve, s_stats2, i - 1)
                    waited(dve)
                    v.bn_stats(bn2[:], tile_of(xs, i - 1)).then_inc(s_bn2, 1)
                    dve.wait_ge(s_bn2, i)
                    at_least(dve, s_const2, i - 1)
                    waited(dve)
                    v.bn_aggr(mv2[:], bn2[:]).then_inc(s_stats2, 1)
                if has(i):
                    rest(gT_lo, ps_gT, gT_hi, s_gT_hi, s_gT_lo, i)
                if isinstance(i, int) and i == 0:
                    for b in range(KD):
                        dve.wait_ge(s_row_abs, b + 1)
                        v.tensor_scalar(abs_bc[:, b], ones[:], row_abs[:, b:b + 1], 2.0 / D, ALU.mult, ALU.mult)\
                         .then_inc(s_abs_bc, 1)
                if isinstance(i, int) and i == LOOP_FROM - 1:
                    dve.wait_ge(s_x_rest, 16 * (NT - EARLY))

            stats1(0)
            prep_lo(0)
            rest(hT_lo, ps_hT, hT_hi, s_hT_hi, s_hT_lo, 0)
            stats1(1)
            stats1(2)
            iterate(dve, body)

        @block.tensor
        def _(pe):
            t = nc.tensor
            pe.wait_ge(s_masks, 6)
            pe.wait_ge(s_route, R["onehot"])
            flat = onehot[:].rearrange("p e c -> p (e c)")
            t.matmul(ps_chunk_sum, flat, ones_col[:, 0:1], start=True, stop=True).then_inc(s_onehot_ps, 1)
            t.matmul(ps_rank, before[:], flat[:, 0:E * NC], start=True, stop=False)
            pe.wait_ge(s_route, R["chunk_sum"])
            t.matmul(ps_rank, chunk_sum[:], chunk_before[:].rearrange("p e c -> p (e c)"), start=False, stop=True)
            t.matmul(ps_total, chunk_sum[:], chunk_of[:], start=True, stop=True).then_inc(s_rank_ps, 1)
            pe.wait_ge(s_route, R["tile_val"])
            for c in range(NC):
                last = t.matmul(ps_slot, lane_hot[:, c], tile_val[:, c], start=(c == 0), stop=(c == NC - 1))
            last.then_inc(s_slot_ps, 1)

            def transpose(ps, src):
                for b in range(KD):
                    last = t.transpose(ps[:, b * P:(b + 1) * P], src(b), ident[:])
                return last

            def prep(w):
                pe.wait_ge(s_nat[w], 16)
                for k in range(KD):
                    n = prep_no[w, k]
                    at_least(pe, s_prep_lo, n - 1)
                    transpose(ps_prep[n % 2], lambda b: nat[:, w, b, k * P:(k + 1) * P]).then_inc(s_prep_ps, 1)

            def transpose1(j):
                at_least(pe, s_h, j + 1)
                at_least(pe, s_hT_lo, j)
                transpose(ps_hT, lambda b: h[:, b * P:(b + 1) * P]).then_inc(s_hT_ps, 1)

            def product(ps, hi, lo, expert):
                for k in range(KD):
                    blk = slice(k * P, (k + 1) * P)
                    c_hi = ct_hi[:, bass.ds(expert * (KD * D) + k * D, D)]
                    c_lo = ct_lo[:, bass.ds(expert * (KD * D) + k * D, D)]
                    t.matmul(ps[:], hi[:, blk], c_hi, start=(k == 0), stop=False)
                    t.matmul(ps[:], hi[:, blk], c_lo, start=False, stop=False)
                    last = t.matmul(ps[:], lo[:, blk], c_hi, start=False, stop=(k == KD - 1))
                return last

            def expert(j):
                return pe.value_load(expert_of[0:1, bass.ds(j, 1)], min_val=0, max_val=E - 1)

            def body(i):
                if has(i):
                    at_least(pe, s_hT_lo, i + 1)
                    at_least(pe, s_gu, i)
                    if isinstance(i, int) and i < E:
                        pe.wait_ge(s_prep_lo, prep_no[i, KD - 1] + 1)
                    product(ps_z, hT_hi, hT_lo, expert(i)).then_inc(s_z, 1)
                if has(i - 2):
                    at_least(pe, s_h2, i - 1)
                    at_least(pe, s_h2T_lo, i - 2)
                    transpose(ps_h2T, lambda b: h2[:, b * P:(b + 1) * P]).then_inc(s_h2T_ps, 1)
                if has(i + 1):
                    transpose1(i + 1)
                if isinstance(i, int) and i in PREPS:
                    for w in PREPS[i]:
                        prep(w)
                if has(i - 1):
                    at_least(pe, s_gT_lo, i)
                    at_least(pe, s_x1, i - 1)
                    product(ps_y, gT_hi, gT_lo, expert(i - 1)).then_inc(s_y, 1)
                if has(i):
                    at_least(pe, s_gu, i + 1)
                    at_least(pe, s_gT_lo, i)
                    transpose(ps_gT, lambda b: gu[:, b * P:(b + 1) * P]).then_inc(s_gT_ps, 1)
                if isinstance(i, int) and i == 0:
                    pe.wait_ge(s_abs_bc, KD)
                    for b in range(KD):
                        last = t.matmul(ps_m[:, b * P:(b + 1) * P], abs_bc[:, b], ident[:], start=True, stop=True)
                    last.then_inc(s_alpha_ps, 1)
                if has(i - 2):
                    if isinstance(i, int) and i == 2:
                        pe.wait_ge(s_alpha, 1)
                    at_least(pe, s_h2T_lo, i - 1)
                    at_least(pe, s_scaled, i - 2)
                    for k in range(KD):
                        blk = slice(k * P, (k + 1) * P)
                        t.matmul(ps_m[:], h2T_hi[:, blk], half_sign[:, k], start=(k == 0), stop=False)
                        last = t.matmul(ps_m[:], h2T_lo[:, blk], half_sign[:, k], start=False, stop=(k == KD - 1))
                    last.then_inc(s_m, 1)

            pe.wait_ge(s_ident, 1)
            prep(0)
            transpose1(0)
            pe.wait_ge(s_expert, 1)
            iterate(pe, body)


def kernel(x, itok_BxS_13_99985, ctx_2048, L0_ffn_weight, L0_ffn_bias):
    import numpy as np
    import concourse.bacc as bacc
    from concourse.bass_utils import run_bass_kernel_spmd

    given = {"x": np.ascontiguousarray(x).reshape(T, D), "token_ids": np.ascontiguousarray(itok_BxS_13_99985).reshape(T),
             "ctx_w": np.ascontiguousarray(ctx_2048), "weight": np.ascontiguousarray(L0_ffn_weight),
             "bias": np.ascontiguousarray(L0_ffn_bias)}
    nc = bacc.Bacc("TRN2", target_bir_lowering=False, num_devices=1)
    args = [nc.dram_tensor(f"in_{n}", a.shape, mybir.dt.from_np(a.dtype), kind="ExternalInput").ap()
            for n, a in given.items()]
    out = nc.dram_tensor("out_rows_dram", (T, D), mybir.dt.float32, kind="ExternalOutput").ap()
    xattn_ffn(nc, *args, out)
    r = run_bass_kernel_spmd(nc, [{f"in_{n}": a for n, a in given.items()}], core_ids=[0])
    return r.results[0]["out_rows_dram"].reshape(4, 512, D)
```

```python
from contextlib import ExitStack

import concourse.bass as bass
from concourse import mybir

P = 128
D = 512
KD = D // P
E = 4
VOCAB = 25000
PER_EXPERT = VOCAB // E
T = 4 * 512
NC = T // P
NT = NC + E - 1
NTP = NT + 1
EPS = 1e-5

POOL_CHUNKS = 3
LOOP_FROM, LOOP_TO = 4, NT - 3
LAST = NT + 2


def xattn_ffn(nc, x, token_ids, ctx_w, weight, bias, out):
    f32, f32r, f16, i32 = mybir.dt.float32, mybir.dt.float32r, mybir.dt.float16, mybir.dt.int32
    ALU, ACT, AX = mybir.AluOpType, mybir.ActivationFunctionType, mybir.AxisListType

    ctx = ExitStack()
    with ctx:
        def sb(name, shape, dt=f32):
            return ctx.enter_context(nc.sbuf_tensor(name, shape, dt))

        def sem(name):
            return ctx.enter_context(nc.semaphore(name))

        def bank(name):
            return ctx.enter_context(nc.psum_tensor(name, [P, D], f32))

        ps_hT, ps_z, ps_gT, ps_y = bank("ps_hT"), bank("ps_z"), bank("ps_gT"), bank("ps_y")
        ps_h2T, ps_m = bank("ps_h2T"), bank("ps_m")
        ps_prep = [bank("ps_prep0"), bank("ps_prep1")]
        ps_rank, ps_chunk_sum, ps_total, ps_slot = ps_y[:, 0:E * NC], ps_m[:, 0:1], ps_h2T[:, 0:E], ps_hT[:, 0:NTP]

        nat = sb("nat", [P, E + 1, KD, D])
        ct_hi = sb("ct_hi", [P, E * KD * D], f32r)
        ct_lo = sb("ct_lo", [P, E * KD * D], f32r)
        half_sign = sb("half_sign", [P, KD, D], f32r)
        alpha2 = sb("alpha2", [P, D])
        bias_bc = sb("bias_bc", [P, D])
        ident = sb("ident", [P, P])
        ones = sb("ones", [P, P])
        before = sb("before", [P, P], f16)
        ones_col = sb("ones_col", [P, 2], f16)
        chunk_before = sb("chunk_before", [P, E, NC], f16)
        chunk_of = sb("chunk_of", [P, E], f16)
        iota_lane = sb("iota_lane", [P, P], f16)
        iota_tile = sb("iota_tile", [P, NTP])
        iota_128 = sb("iota_128", [P, NC])
        token_no = sb("token_no", [P, NC])
        dropped = sb("dropped", [P, 1])
        minus_half = sb("minus_half", [P, 1])
        tid = sb("tid", [P, NC], i32)
        reached = sb("reached", [P, E + 1, NC])
        onehot = sb("onehot", [P, 2 * E, NC], f16)
        chunk_sum = sb("chunk_sum", [P, P], f16)
        full = sb("full", [P, E, NC])
        tiles_of = sb("tiles_of", [P, E])
        tile_from = sb("tile_from", [P, E])
        rank = sb("rank", [P, E, NC])
        rank1 = sb("rank1", [P, E, NC])
        slot = sb("slot", [P, NC], i32)
        lane_i, tile_i = sb("lane_i", [P, NC], i32), sb("tile_i", [P, NC], i32)
        lane, tile = sb("lane", [P, NC]), sb("tile", [P, NC])
        lane_hot = sb("lane_hot", [P, NC, P], f16)
        tile_hot = sb("tile_hot", [P, NC, NTP])
        tile_val = sb("tile_val", [P, NC, NTP], f16)
        is_empty = sb("is_empty", [P, NTP])
        gather_idx = sb("gather_idx", [P, NTP], i32)
        scatter_idx = sb("scatter_idx", [P, NTP], i32)
        at_least_e = sb("at_least_e", [P, E - 1, NTP])
        expert_of = sb("expert_of", [P, NTP], i32)
        xs = sb("xs", [P, NT * D])
        bn1, bn2 = sb("bn1", [P, 6]), sb("bn2", [P, 6])
        mv1, mv2 = sb("mv1", [P, 2]), sb("mv2", [P, 2])
        var1, var2 = sb("var1", [P, 1]), sb("var2", [P, 1])
        rs1, rs2 = sb("rs1", [P, 1]), sb("rs2", [P, 1])
        nm1, nm2 = sb("nm1", [P, 1]), sb("nm2", [P, 1])
        h, h2 = sb("h", [P, D]), sb("h2", [P, D])
        hT_hi, hT_lo = sb("hT_hi", [P, D], f32r), sb("hT_lo", [P, D], f32r)
        silu, gu = sb("silu", [P, D]), sb("gu", [P, D])
        gT_hi, gT_lo = sb("gT_hi", [P, D], f32r), sb("gT_lo", [P, D], f32r)
        h2T_hi, h2T_lo = sb("h2T_hi", [P, D], f32r), sb("h2T_lo", [P, D], f32r)
        scaled = sb("scaled", [P, D])
        row_abs = sb("row_abs", [P, KD])
        abs_bc = sb("abs_bc", [P, KD, P])
        out_rows = [sb("out_rows0", [P, D]), sb("out_rows1", [P, D])]
        out_idx = [sb("out_idx0", [P, 1], i32), sb("out_idx1", [P, 1], i32)]

        s_stats1, s_const1, s_h = sem("s_stats1"), sem("s_const1"), sem("s_h")
        s_hT_ps, s_hT_hi, s_hT_lo = sem("s_hT_ps"), sem("s_hT_hi"), sem("s_hT_lo")
        s_z, s_silu, s_gu = sem("s_z"), sem("s_silu"), sem("s_gu")
        s_gT_ps, s_gT_hi, s_gT_lo = sem("s_gT_ps"), sem("s_gT_hi"), sem("s_gT_lo")
        s_y, s_x1, s_stats2, s_const2, s_h2 = sem("s_y"), sem("s_x1"), sem("s_stats2"), sem("s_const2"), sem("s_h2")
        s_h2T_ps, s_h2T_hi, s_h2T_lo = sem("s_h2T_ps"), sem("s_h2T_hi"), sem("s_h2T_lo")
        s_m, s_scaled, s_xb, s_out = sem("s_m"), sem("s_scaled"), sem("s_xb"), sem("s_out")
        s_bn1, s_bn2 = sem("s_bn1"), sem("s_bn2")
        s_var1, s_rs1 = sem("s_var1"), sem("s_rs1")
        s_var2, s_rs2 = sem("s_var2"), sem("s_rs2")
        s_out_idx = sem("s_out_idx")
        s_scattered = [sem("s_scattered0"), sem("s_scattered1")]
        EARLY = LOOP_FROM + 3
        s_x = [sem(f"s_rows{j}") for j in range(EARLY)]
        s_x_rest = sem("s_rows_rest")
        s_tid, s_bias = sem("s_tid"), sem("s_bias")
        s_nat = [sem(f"s_nat{w}") for w in range(E + 1)]
        s_ident, s_mask0, s_masks, s_iotas = sem("s_ident"), sem("s_mask0"), sem("s_masks"), sem("s_iotas")
        s_prep_ps, s_prep_hi, s_prep_lo = sem("s_prep_ps"), sem("s_prep_hi"), sem("s_prep_lo")
        s_row_abs, s_abs_bc, s_alpha_ps, s_alpha = sem("s_row_abs"), sem("s_abs_bc"), sem("s_alpha_ps"), sem("s_alpha")
        s_lane_hot = sem("s_lane_hot")
        s_table = sem("s_table")
        s_waited = sem("s_waited")
        s_route = sem("s_route")
        s_onehot_ps, s_rank_ps, s_slot_ps = sem("s_onehot_ps"), sem("s_rank_ps"), sem("s_slot_ps")
        s_gather_idx, s_scatter_idx, s_expert = sem("s_gather_idx"), sem("s_scatter_idx"), sem("s_expert")

        R = {name: n + 1 for n, name in enumerate((
            "zeroed", "reached0", "reached_end", "reached1", "reached2", "reached3", "onehot", "chunk_sum",
            "full", "tiles0", "tiles_of", "from0", "from1", "from2", "from3", "shifted", "masked", "slot",
            "lane_i", "tile_i", "lane", "tile", "lane_hot", "tile_hot", "tile_val", "empty", "at_least"))}

        WEIGHT = E
        PREPS = {0: 2, 1: 3, 2: WEIGHT}
        EARLY_BLOCKS, LATE_BLOCKS = range(3), range(3, KD)
        FIRST_HALF, SECOND_HALF = range(KD // 2), range(KD // 2, KD)
        prep_order = [(w, k) for w in (0, 1, *PREPS.values()) for k in range(KD)]
        prep_no = {wk: n for n, wk in enumerate(prep_order)}

        prep_banks = [*ps_prep, ps_z, ps_gT,  *ps_prep, ps_y, ps_m,  *ps_prep, ps_y, ps_m,
                      *ps_prep, ps_m, ps_h2T,  *ps_prep, ps_m, ps_prep[0]]

        def prep_out(n, bank):
            return max((m + 1 for m in range(n) if prep_banks[m] is bank), default=0)

        def tile_of(buf, j):
            return buf[:, bass.ds(j * D, D)]

        def has(j):
            return not isinstance(j, int) or 0 <= j < NT

        def at_least(eng, s, n):
            if not isinstance(n, int) or n > 0:
                eng.wait_ge(s, n)

        def waited(eng):
            eng.sem_inc(s_waited, 1)

        def iterate(eng, body):
            for i in range(0, LOOP_FROM):
                body(i)
            with eng.Fori(LOOP_FROM, LOOP_TO) as i:
                body(i)
            for i in range(LOOP_TO, LAST + 1):
                body(i)

        block = ctx.enter_context(nc.Block())

        @block.sync
        def _(sp):
            sp.dma_start(tid[:], token_ids.rearrange("(p c) -> p c", p=P)).then_inc(s_tid, 16)
            for w in (0, 1, 2, 3, WEIGHT):
                if w == 3:
                    sp.wait_ge(s_x[2], 16)
                src = weight if w == WEIGHT else ctx_w[w]
                sp.dma_start(nat[:, w], src.rearrange("(b p) d -> p b d", p=P)).then_inc(s_nat[w], 16)
            sp.dma_start(bias_bc[:], bias.partition_broadcast(P)).then_inc(s_bias, 16)

        @block.gpsimd
        def _(pool):
            g = nc.gpsimd
            g.memset(ident[:], 0.0).then_inc(s_mask0, 1)
            g.memset(before[:], 1.0).then_inc(s_mask0, 1)
            g.memset(chunk_before[:], 1.0).then_inc(s_mask0, 1)
            g.memset(chunk_of[:], 1.0).then_inc(s_mask0, 1)
            g.memset(ones_col[:], 1.0).then_inc(s_masks, 1)
            g.memset(minus_half[:], -0.5).then_inc(s_masks, 1)
            pool.wait_ge(s_mask0, 4)
            g.affine_select(out=before[:], in_=before[:], compare_op=ALU.is_gt, fill=0.0, base=0,
                            pattern=[[1, P]], channel_multiplier=-1).then_inc(s_masks, 1)
            g.affine_select(out=chunk_before[:], in_=chunk_before[:], compare_op=ALU.is_gt, fill=0.0, base=0,
                            pattern=[[NC, E], [1, NC]], channel_multiplier=-1).then_inc(s_mask0, 1)
            g.affine_select(out=chunk_of[:], in_=chunk_of[:], compare_op=ALU.is_ge, fill=0.0, base=0,
                            pattern=[[-NC, E]], channel_multiplier=1).then_inc(s_mask0, 1)
            g.affine_select(out=ident[:], in_=ident[:], compare_op=ALU.not_equal, fill=1.0, base=0,
                            pattern=[[-1, P]], channel_multiplier=1).then_inc(s_ident, 1)
            pool.wait_ge(s_mask0, 6)
            g.affine_select(out=chunk_before[:], in_=chunk_before[:], compare_op=ALU.is_ge, fill=0.0, base=0,
                            pattern=[[-NC, E], [0, NC]], channel_multiplier=1).then_inc(s_masks, 1)
            g.affine_select(out=chunk_of[:], in_=chunk_of[:], compare_op=ALU.is_ge, fill=0.0, base=NC - 1,
                            pattern=[[NC, E]], channel_multiplier=-1).then_inc(s_masks, 1)
            g.iota(iota_128[:], pattern=[[P, NC]], base=0, channel_multiplier=0,
                   allow_small_or_imprecise_dtypes=True).then_inc(s_iotas, 1)
            g.iota(iota_lane[:], pattern=[[1, P]], base=0, channel_multiplier=0,
                   allow_small_or_imprecise_dtypes=True).then_inc(s_iotas, 1)
            g.iota(iota_tile[:], pattern=[[1, NTP]], base=0, channel_multiplier=0,
                   allow_small_or_imprecise_dtypes=True).then_inc(s_iotas, 1)
            g.iota(token_no[:], pattern=[[1, NC]], base=1, channel_multiplier=NC,
                   allow_small_or_imprecise_dtypes=True).then_inc(s_iotas, 1)
            g.iota(dropped[:], pattern=[[1, 1]], base=1 + T, channel_multiplier=1,
                   allow_small_or_imprecise_dtypes=True).then_inc(s_iotas, 1)

            def gather(j):
                pool.indirect_dma_start(
                    out=xs[:, j * D:(j + 1) * D], out_offset=None, in_=x,
                    in_offset=bass.IndirectOffsetOnAxis(ap=gather_idx[:, j:j + 1], axis=0),
                    bounds_check=T - 1, oob_is_err=False).then_inc(s_x[j] if j < EARLY else s_x_rest, 16)

            def constants(j, mv, var, rs, nm, s_stats, s_var, s_rs, s_done, s_used):
                at_least(pool, s_stats, j + 1)
                waited(pool)
                g.tensor_scalar(var[:], mv[:, 1:2], EPS, None, ALU.add).then_inc(s_var, 1)
                pool.wait_ge(s_var, j + 1)
                at_least(pool, s_used, j)
                g.tensor_tensor(rs[:], var[:], minus_half[:], ALU.pow).then_inc(s_rs, 1)
                pool.wait_ge(s_rs, j + 1)
                waited(pool)
                g.tensor_scalar(nm[:], mv[:, 0:1], rs[:], -1.0, ALU.mult, ALU.mult).then_inc(s_done, 1)

            def constants1(j):
                constants(j, mv1, var1, rs1, nm1, s_stats1, s_var1, s_rs1, s_const1, s_h)

            def finish(j, half):
                if not isinstance(j, int) or j >= 2:
                    pool.wait_ge(s_scattered[half], (j - half) * 8)
                g.tensor_copy(out_idx[half][:], scatter_idx[:, bass.ds(j, 1)]).then_inc(s_out_idx, 1)
                if not isinstance(j, int) or j < NT - 1:
                    at_least(pool, s_scaled, j + 1)
                    at_least(pool, s_xb, j + 1)
                    g.tensor_tensor(out_rows[half][:], tile_of(xs, j), scaled[:], ALU.add).then_inc(s_out, 1)
                pool.wait_ge(s_out, j + 1)
                pool.wait_ge(s_out_idx, j + 1)
                waited(pool)
                pool.indirect_dma_start(
                    out=out, out_offset=bass.IndirectOffsetOnAxis(ap=out_idx[half][:], axis=0),
                    in_=out_rows[half][:], in_offset=None,
                    bounds_check=T - 1, oob_is_err=False).then_inc(s_scattered[half], 16)

            pool.wait_ge(s_route, R["tile"])
            for c in range(NC - POOL_CHUNKS, NC):
                last = g.tensor_scalar(lane_hot[:, c], iota_lane[:], lane[:, c:c + 1], None, ALU.is_equal)
            last.then_inc(s_lane_hot, 1)
            pool.wait_ge(s_gather_idx, 1)
            for j in range(3):
                gather(j)
            constants1(0)
            gather(3)
            constants1(1)
            gather(4)
            gather(5)
            pool.wait_ge(s_bias, 16)

            def body(i, half):
                if has(i + 2):
                    constants1(i + 2)
                if has(i - 3):
                    if isinstance(i, int) and i == 3:
                        pool.wait_ge(s_scatter_idx, 1)
                    finish(i - 3, 1 - half)
                if isinstance(i, int) and i < LOOP_FROM:
                    for j in range(6 + i * 4, min(NT, 10 + i * 4)):
                        gather(j)
                if has(i - 1):
                    constants(i - 1, mv2, var2, rs2, nm2, s_stats2, s_var2, s_rs2, s_const2, s_h2)
                    at_least(pool, s_h2, i)
                    g.tensor_tensor(tile_of(xs, i - 1), tile_of(xs, i - 1), bias_bc[:], ALU.add).then_inc(s_xb, 1)

            for i in range(0, LOOP_FROM):
                body(i, i % 2)
            with pool.Fori(LOOP_FROM, LOOP_TO, 2) as i:
                body(i, 0)
                body(i + 1, 1)
            for i in range(LOOP_TO, LAST + 1):
                body(i, i % 2)
            pool.wait_ge(s_scattered[0], 16 * ((NT + 1) // 2))
            pool.wait_ge(s_scattered[1], 16 * (NT // 2))

        @block.scalar
        def _(act):
            a = nc.scalar

            def prep_hi(w, blocks=range(KD)):
                if w == WEIGHT:
                    return
                for k in blocks:
                    n = prep_no[w, k]
                    act.wait_ge(s_prep_ps, n + 1)
                    at = (w * KD + k) * D
                    a.activation(ct_hi[:, at:at + D], prep_banks[n][:], ACT.Copy).then_inc(s_prep_hi, 1)

            def norm1(j):
                at_least(act, s_const1, j + 1)
                at_least(act, s_hT_ps, j)
                a.activation(h[:], tile_of(xs, j), ACT.Identity, bias=nm1[:], scale=rs1[:]).then_inc(s_h, 1)

            def body(i):
                if has(i):
                    if isinstance(i, int) and i == 0:
                        act.wait_ge(s_table, 1)
                    at_least(act, s_z, i + 1)
                    a.activation(silu[:], ps_z[:], ACT.Silu).then_inc(s_silu, 1)
                if has(i - 2):
                    at_least(act, s_h2T_ps, i - 1)
                    at_least(act, s_m, i - 2)
                    a.activation(h2T_hi[:], ps_h2T[:], ACT.Copy).then_inc(s_h2T_hi, 1)
                if has(i + 1):
                    at_least(act, s_hT_ps, i + 2)
                    a.activation(hT_hi[:], ps_hT[:], ACT.Copy).then_inc(s_hT_hi, 1)
                if isinstance(i, int) and i in PREPS:
                    prep_hi(PREPS[i])
                if has(i + 2):
                    norm1(i + 2)
                if has(i):
                    at_least(act, s_gT_ps, i + 1)
                    a.activation(gT_hi[:], ps_gT[:], ACT.Copy).then_inc(s_gT_hi, 1)
                if has(i - 1):
                    at_least(act, s_const2, i)
                    at_least(act, s_h2T_ps, i - 1)
                    a.activation(h2[:], tile_of(xs, i - 1), ACT.Identity, bias=nm2[:], scale=rs2[:]).then_inc(s_h2, 1)
                if isinstance(i, int) and i == 0:
                    act.wait_ge(s_nat[WEIGHT], 16)
                    for b in range(KD):
                        a.activation(silu[:], nat[:, WEIGHT, b], ACT.Abs,
                                     accum_out=row_abs[:, b:b + 1]).then_inc(s_row_abs, 1)
                        act.wait_ge(s_row_abs, b + 1)
                if isinstance(i, int) and i == 2:
                    act.wait_ge(s_alpha_ps, 1)
                    a.activation(alpha2[:], ps_prep[1][:], ACT.Copy).then_inc(s_alpha, 1)

            act.wait_ge(s_route, R["reached0"])
            a.activation(silu[:, 0:1], ones[:, 0:1], ACT.Silu).then_inc(s_table, 1)
            prep_hi(0)
            prep_hi(1, FIRST_HALF)
            norm1(0)
            act.wait_ge(s_hT_ps, 1)
            a.activation(hT_hi[:], ps_hT[:], ACT.Copy).then_inc(s_hT_hi, 1)
            norm1(1)
            prep_hi(1, SECOND_HALF)
            iterate(act, body)

        @block.vector
        def _(dve):
            v = nc.vector
            v.memset(ones[:], 1.0).then_inc(s_route, 1)

            def step(name, ins):
                ins.then_inc(s_route, 1)

            def after(name):
                dve.wait_ge(s_route, R[name])

            step("reached0", v.memset(reached[:, 0], 1.0))
            step("reached_end", v.memset(reached[:, E], 0.0))
            dve.wait_ge(s_tid, 16)
            for e in range(1, E):
                step(f"reached{e}", v.tensor_scalar(reached[:, e], tid[:], float(PER_EXPERT * e), None, ALU.is_ge))
            v.memset(onehot[:, E:2 * E], 0.0).then_inc(s_masks, 1)
            after("reached3")
            step("onehot", v.tensor_tensor(onehot[:, 0:E], reached[:, 0:E], reached[:, 1:E + 1], ALU.subtract))
            dve.wait_ge(s_onehot_ps, 1)
            step("chunk_sum", v.tensor_scalar(chunk_sum[:], ones[:], ps_chunk_sum, None, ALU.mult))
            dve.wait_ge(s_iotas, 5)
            dve.wait_ge(s_rank_ps, 1)
            step("full", v.tensor_tensor(full[:], ps_total.unsqueeze(2).broadcast_to([P, E, NC]),
                                         iota_128[:].unsqueeze(1).broadcast_to([P, E, NC]), ALU.is_gt))
            after("full")
            step("tiles0", v.tensor_reduce(tiles_of[:], full[:], AX.X, ALU.add))
            after("tiles0")
            step("tiles_of", v.tensor_scalar(tiles_of[:], tiles_of[:], 1.0, None, ALU.max))
            step("from0", v.memset(tile_from[:, 0:1], 0.0))
            for e in range(1, E):
                after(f"from{e - 1}")
                step(f"from{e}", v.tensor_tensor(tile_from[:, e:e + 1], tile_from[:, e - 1:e],
                                                 tiles_of[:, e - 1:e], ALU.add))
            after("from3")
            step("shifted", v.scalar_tensor_tensor(
                out=rank1[:], in0=tile_from[:].unsqueeze(2).broadcast_to([P, E, NC]), scalar=float(P),
                in1=ps_rank.rearrange("p (e c) -> p e c", e=E), op0=ALU.mult, op1=ALU.add))
            after("shifted")
            step("masked", v.tensor_tensor(rank[:], rank1[:], onehot[:, 0:E], ALU.mult))
            after("masked")
            with nc.allow_low_precision(reason="whole numbers below 2^12"):
                step("slot", v.tensor_reduce(slot[:], rank[:].rearrange("p e c -> p c e"), AX.X, ALU.add))
            after("slot")
            step("lane_i", v.tensor_scalar(lane_i[:], slot[:], P - 1, None, ALU.bitwise_and))
            step("tile_i", v.tensor_scalar(tile_i[:], slot[:], P.bit_length() - 1, None, ALU.logical_shift_right))
            after("tile_i")
            step("lane", v.tensor_copy(lane[:], lane_i[:]))
            step("tile", v.tensor_copy(tile[:], tile_i[:]))
            after("tile")
            for c in range(NC - POOL_CHUNKS):
                last = v.tensor_scalar(lane_hot[:, c], iota_lane[:], lane[:, c:c + 1], None, ALU.is_equal)
            step("lane_hot", last)
            step("tile_hot", v.tensor_tensor(tile_hot[:], tile[:].unsqueeze(2).broadcast_to([P, NC, NTP]),
                                             iota_tile[:].unsqueeze(1).broadcast_to([P, NC, NTP]), ALU.is_equal))
            after("tile_hot")
            step("tile_val", v.tensor_tensor(tile_val[:], tile_hot[:],
                                             token_no[:].unsqueeze(2).broadcast_to([P, NC, NTP]), ALU.mult))
            dve.wait_ge(s_slot_ps, 1)
            v.tensor_scalar(gather_idx[:], ps_slot, 1.0, 0.0, ALU.subtract, ALU.max).then_inc(s_gather_idx, 1)
            step("empty", v.tensor_scalar(is_empty[:], ps_slot, 0.0, dropped[:], ALU.is_equal, ALU.mult))
            step("at_least", v.tensor_tensor(at_least_e[:], iota_tile[:].unsqueeze(1).broadcast_to([P, E - 1, NTP]),
                                             tile_from[:, 1:E].unsqueeze(2).broadcast_to([P, E - 1, NTP]), ALU.is_ge))
            after("at_least")
            v.scalar_tensor_tensor(out=scatter_idx[:], in0=ps_slot, scalar=-1.0, in1=is_empty[:],
                                   op0=ALU.add, op1=ALU.add).then_inc(s_scatter_idx, 1)
            with nc.allow_low_precision(reason="whole numbers below 4"):
                v.tensor_reduce(expert_of[:], at_least_e[:].rearrange("p e t -> p t e"), AX.X, ALU.add)\
                 .then_inc(s_expert, 1)

            def prep_lo(w, blocks=range(KD)):
                for k in blocks:
                    n = prep_no[w, k]
                    if w == WEIGHT:
                        dve.wait_ge(s_prep_ps, n + 1)
                        v.tensor_scalar(half_sign[:, k], prep_banks[n][:], 0.0, -0.5, ALU.is_ge, ALU.add)\
                         .then_inc(s_prep_lo, 1)
                    else:
                        dve.wait_ge(s_prep_hi, sum(o[0] != WEIGHT for o in prep_order[:n + 1]))
                        at = (w * KD + k) * D
                        v.tensor_tensor(ct_lo[:, at:at + D], prep_banks[n][:], ct_hi[:, at:at + D].bitcast(f32),
                                        ALU.subtract).then_inc(s_prep_lo, 1)

            def stats1(j):
                if isinstance(j, int) and j < EARLY:
                    dve.wait_ge(s_x[j], 16)
                at_least(dve, s_stats1, j)
                waited(dve)
                v.bn_stats(bn1[:], tile_of(xs, j)).then_inc(s_bn1, 1)
                dve.wait_ge(s_bn1, j + 1)
                at_least(dve, s_const1, j)
                waited(dve)
                v.bn_aggr(mv1[:], bn1[:]).then_inc(s_stats1, 1)

            def rest(lo, ps, hi, s_hi, s_lo, j):
                at_least(dve, s_hi, j + 1)
                v.tensor_tensor(lo[:], ps[:], hi[:].bitcast(f32), ALU.subtract).then_inc(s_lo, 1)

            def residual(j):
                at_least(dve, s_y, j + 1)
                v.tensor_tensor(tile_of(xs, j), ps_y[:], tile_of(xs, j), ALU.add).then_inc(s_x1, 1)

            def stats2(j):
                dve.wait_ge(s_x1, j + 1)
                at_least(dve, s_stats2, j)
                waited(dve)
                v.bn_stats(bn2[:], tile_of(xs, j)).then_inc(s_bn2, 1)
                dve.wait_ge(s_bn2, j + 1)
                at_least(dve, s_const2, j)
                waited(dve)
                v.bn_aggr(mv2[:], bn2[:]).then_inc(s_stats2, 1)

            def body(i):
                last_tile_first = isinstance(i, int) and i == NT
                if has(i - 3):
                    if isinstance(i, int) and i == 3:
                        dve.wait_ge(s_alpha, 1)
                    at_least(dve, s_m, i - 2)
                    at_least(dve, s_out, i - 3)
                    v.tensor_tensor(scaled[:], ps_m[:], alpha2[:], ALU.mult).then_inc(s_scaled, 1)
                if isinstance(i, int) and i - 3 == NT - 1:
                    half = (NT - 1) % 2
                    dve.wait_ge(s_scaled, NT)
                    dve.wait_ge(s_xb, NT)
                    dve.wait_ge(s_scattered[half], 16 * ((NT - 1) // 2))
                    v.tensor_tensor(out_rows[half][:], tile_of(xs, NT - 1), scaled[:], ALU.add).then_inc(s_out, 1)
                if isinstance(i, int) and i == 2:
                    for b in range(KD):
                        dve.wait_ge(s_row_abs, b + 1)
                        v.tensor_scalar(abs_bc[:, b], ones[:], row_abs[:, b:b + 1], 2.0 / D, ALU.mult, ALU.mult)\
                         .then_inc(s_abs_bc, 1)
                if has(i):
                    at_least(dve, s_silu, i + 1)
                    at_least(dve, s_gT_ps, i)
                    v.tensor_tensor(gu[:], ps_z[:], silu[:], ALU.mult).then_inc(s_gu, 1)
                if last_tile_first:
                    residual(i - 1)
                    stats2(i - 1)
                if isinstance(i, int) and PREPS.get(i) == WEIGHT:
                    prep_lo(WEIGHT, EARLY_BLOCKS)
                if has(i - 2):
                    rest(h2T_lo, ps_h2T, h2T_hi, s_h2T_hi, s_h2T_lo, i - 2)
                if has(i + 1):
                    rest(hT_lo, ps_hT, hT_hi, s_hT_hi, s_hT_lo, i + 1)
                if isinstance(i, int) and i in PREPS:
                    prep_lo(PREPS[i], LATE_BLOCKS if PREPS[i] == WEIGHT else range(KD))
                if has(i + 3):
                    stats1(i + 3)
                if has(i - 1) and not last_tile_first:
                    residual(i - 1)
                    stats2(i - 1)
                if has(i):
                    rest(gT_lo, ps_gT, gT_hi, s_gT_hi, s_gT_lo, i)
                if isinstance(i, int) and i == LOOP_FROM - 1:
                    dve.wait_ge(s_x_rest, 16 * (NT - EARLY))

            prep_lo(0)
            stats1(0)
            prep_lo(1, FIRST_HALF)
            stats1(1)
            rest(hT_lo, ps_hT, hT_hi, s_hT_hi, s_hT_lo, 0)
            prep_lo(1, SECOND_HALF)
            stats1(2)
            iterate(dve, body)

        @block.tensor
        def _(pe):
            t = nc.tensor
            pe.wait_ge(s_masks, 6)
            pe.wait_ge(s_route, R["onehot"])
            flat = onehot[:].rearrange("p e c -> p (e c)")
            t.matmul(ps_chunk_sum, flat, ones_col[:, 0:1], start=True, stop=True).then_inc(s_onehot_ps, 1)
            t.matmul(ps_rank, before[:], flat[:, 0:E * NC], start=True, stop=False)
            pe.wait_ge(s_route, R["chunk_sum"])
            t.matmul(ps_rank, chunk_sum[:], chunk_before[:].rearrange("p e c -> p (e c)"), start=False, stop=True)
            t.matmul(ps_total, chunk_sum[:], chunk_of[:], start=True, stop=True).then_inc(s_rank_ps, 1)

            def transpose(ps, src):
                for b in range(KD):
                    last = t.transpose(ps[:, b * P:(b + 1) * P], src(b), ident[:])
                return last

            def prep(w, blocks=range(KD)):
                pe.wait_ge(s_nat[w], 16)
                for k in blocks:
                    n = prep_no[w, k]
                    at_least(pe, s_prep_lo, prep_out(n, prep_banks[n]))
                    transpose(prep_banks[n], lambda b: nat[:, w, b, k * P:(k + 1) * P]).then_inc(s_prep_ps, 1)

            def transpose1(j):
                at_least(pe, s_h, j + 1)
                at_least(pe, s_hT_lo, j)
                transpose(ps_hT, lambda b: h[:, b * P:(b + 1) * P]).then_inc(s_hT_ps, 1)

            def product(ps, hi, lo, expert):
                for k in range(KD):
                    blk = slice(k * P, (k + 1) * P)
                    c_hi = ct_hi[:, bass.ds(expert * (KD * D) + k * D, D)]
                    c_lo = ct_lo[:, bass.ds(expert * (KD * D) + k * D, D)]
                    t.matmul(ps[:], hi[:, blk], c_hi, start=(k == 0), stop=False)
                    t.matmul(ps[:], hi[:, blk], c_lo, start=False, stop=False)
                    last = t.matmul(ps[:], lo[:, blk], c_hi, start=False, stop=(k == KD - 1))
                return last

            def expert(j):
                return pe.value_load(expert_of[0:1, bass.ds(j, 1)], min_val=0, max_val=E - 1)

            def transpose2(j):
                at_least(pe, s_h2, j + 1)
                at_least(pe, s_h2T_lo, j)
                transpose(ps_h2T, lambda b: h2[:, b * P:(b + 1) * P]).then_inc(s_h2T_ps, 1)

            def product2(j, e):
                at_least(pe, s_gT_lo, j + 1)
                at_least(pe, s_x1, j)
                product(ps_y, gT_hi, gT_lo, e).then_inc(s_y, 1)

            def body(i):
                e_now = expert(i) if has(i) else None
                e_prev = expert(i - 1) if has(i - 1) else None
                last_tile_first = isinstance(i, int) and i == NT
                if has(i):
                    at_least(pe, s_hT_lo, i + 1)
                    at_least(pe, s_gu, i)
                    if isinstance(i, int) and i < E:
                        pe.wait_ge(s_prep_lo, prep_no[i, KD - 1] + 1)
                    product(ps_z, hT_hi, hT_lo, e_now).then_inc(s_z, 1)
                if last_tile_first:
                    product2(i - 1, e_prev)
                if isinstance(i, int) and PREPS.get(i) == WEIGHT:
                    prep(WEIGHT, EARLY_BLOCKS)
                if has(i - 2):
                    transpose2(i - 2)
                if has(i + 1):
                    transpose1(i + 1)
                if isinstance(i, int) and i in PREPS:
                    prep(PREPS[i], LATE_BLOCKS if PREPS[i] == WEIGHT else range(KD))
                if has(i - 1) and not last_tile_first:
                    product2(i - 1, e_prev)
                if has(i):
                    at_least(pe, s_gu, i + 1)
                    at_least(pe, s_gT_lo, i)
                    transpose(ps_gT, lambda b: gu[:, b * P:(b + 1) * P]).then_inc(s_gT_ps, 1)
                if isinstance(i, int) and i == 2:
                    pe.wait_ge(s_abs_bc, KD)
                    pe.wait_ge(s_prep_lo, prep_out(len(prep_order), ps_prep[1]))
                    for b in range(KD):
                        last = t.matmul(ps_prep[1][:, b * P:(b + 1) * P], abs_bc[:, b], ident[:], start=True, stop=True)
                    last.then_inc(s_alpha_ps, 1)
                if has(i - 2):
                    if isinstance(i, int) and i == 2:
                        pe.wait_ge(s_prep_lo, len(prep_order))
                    at_least(pe, s_h2T_lo, i - 1)
                    at_least(pe, s_scaled, i - 2)
                    for k in range(KD):
                        blk = slice(k * P, (k + 1) * P)
                        t.matmul(ps_m[:], h2T_hi[:, blk], half_sign[:, k], start=(k == 0), stop=False)
                        last = t.matmul(ps_m[:], h2T_lo[:, blk], half_sign[:, k], start=False, stop=(k == KD - 1))
                    last.then_inc(s_m, 1)

            pe.wait_ge(s_ident, 1)
            prep(0)
            pe.wait_ge(s_route, R["tile_val"])
            pe.wait_ge(s_lane_hot, 1)
            for c in range(NC):
                last = t.matmul(ps_slot, lane_hot[:, c], tile_val[:, c], start=(c == 0), stop=(c == NC - 1))
            last.then_inc(s_slot_ps, 1)
            prep(1, FIRST_HALF)
            transpose1(0)
            prep(1, SECOND_HALF)
            pe.wait_ge(s_expert, 1)
            iterate(pe, body)


def kernel(x, itok_BxS_13_99985, ctx_2048, L0_ffn_weight, L0_ffn_bias):
    import numpy as np
    import concourse.bacc as bacc
    from concourse.bass_utils import run_bass_kernel_spmd

    given = {"x": np.ascontiguousarray(x).reshape(T, D), "token_ids": np.ascontiguousarray(itok_BxS_13_99985).reshape(T),
             "ctx_w": np.ascontiguousarray(ctx_2048), "weight": np.ascontiguousarray(L0_ffn_weight),
             "bias": np.ascontiguousarray(L0_ffn_bias)}
    nc = bacc.Bacc("TRN2", target_bir_lowering=False, num_devices=1)
    args = [nc.dram_tensor(f"in_{n}", a.shape, mybir.dt.from_np(a.dtype), kind="ExternalInput").ap()
            for n, a in given.items()]
    out = nc.dram_tensor("out_rows_dram", (T, D), mybir.dt.float32, kind="ExternalOutput").ap()
    xattn_ffn(nc, *args, out)
    r = run_bass_kernel_spmd(nc, [{f"in_{n}": a for n, a in given.items()}], core_ids=[0])
    return r.results[0]["out_rows_dram"].reshape(4, 512, D)
```

```python
from contextlib import ExitStack

import concourse.bass as bass
from concourse import mybir

P = 128
LOG_P = 7
D = 512
KD = D // P
E = 4
VOCAB = 25000
PER_EXPERT = VOCAB // E
T = 4 * 512
NC = T // P
NT = T // P
NI = NT + E - 1
NIP = NI + 1
EPS = 1e-5

POOL_CHUNKS, ACT_CHUNKS = 3, 5
DVE_CHUNKS = NC - POOL_CHUNKS - ACT_CHUNKS
LAG = E + 1
LOOP_FROM, LOOP_TO = LAG + 3, NI - 3
LAST_ITEM, LAST_TILE = NI - 1, NT - 1


def xattn_ffn(nc, x, token_ids, ctx_w, weight, bias, out):
    f32, f32r, f16, i32 = mybir.dt.float32, mybir.dt.float32r, mybir.dt.float16, mybir.dt.int32
    ALU, ACT, AX = mybir.AluOpType, mybir.ActivationFunctionType, mybir.AxisListType

    ctx = ExitStack()
    with ctx:
        def sb(name, shape, dt=f32):
            return ctx.enter_context(nc.sbuf_tensor(name, shape, dt))

        def sem(name):
            return ctx.enter_context(nc.semaphore(name))

        def bank(name):
            return ctx.enter_context(nc.psum_tensor(name, [P, D], f32))

        ps_hT, ps_z, ps_gT, ps_y = bank("ps_hT"), bank("ps_z"), bank("ps_gT"), bank("ps_y")
        ps_h2T, ps_m = bank("ps_h2T"), bank("ps_m")
        ps_prep = [bank("ps_prep0"), bank("ps_prep1")]
        ps_rank, ps_chunk_sum, ps_first, ps_slot = ps_y[:, 0:E * NC], ps_m[:, 0:1], ps_h2T[:, 0:E + 1], ps_hT[:, 0:NT]

        nat = sb("nat", [P, E + 1, KD, D])
        ct_hi = sb("ct_hi", [P, E * KD * D], f32r)
        ct_lo = sb("ct_lo", [P, E * KD * D], f32r)
        sign16 = sb("sign16", [P, KD, D], f16)
        half_sign = sb("half_sign", [P, KD, D], f32r)
        alpha2 = sb("alpha2", [P, D])
        bias_bc = sb("bias_bc", [P, D])
        row_abs = sb("row_abs", [P, KD])
        alpha_dram = nc.dram_tensor("alpha_dram", (D,), f32).ap()
        ident, ident16 = sb("ident", [P, P]), sb("ident16", [P, P], f16)
        ones = sb("ones", [P, P])
        before = sb("before", [P, P], f16)
        expert_before = sb("expert_before", [P, E + 1], f16)
        ones_col = sb("ones_col", [P, 2], f16)
        iota_lane = sb("iota_lane", [P, P], f16)
        iota_item = sb("iota_item", [P, NIP])
        token_no = sb("token_no", [P, NC])
        lane_no = sb("lane_no", [P, 1])
        minus_half = sb("minus_half", [P, 1])
        tid = sb("tid", [P, NC], i32)
        reached = sb("reached", [P, E + 1, NC])
        onehot = sb("onehot", [P, 2 * E, NC], f16)
        chunk_sum = sb("chunk_sum", [P, P], f16)
        rank = sb("rank", [P, E, NC])
        slot = sb("slot", [P, NC], i32)
        lane_i, tile_i = sb("lane_i", [P, NC], i32), sb("tile_i", [P, NC], i32)
        lane, tile = sb("lane", [P, NC]), sb("tile", [P, NC])
        lane_off = sb("lane_off", [P, ACT_CHUNKS, P], f16)
        lane_hot = sb("lane_hot", [P, NC, P], f16)
        tile_hot = sb("tile_hot", [P, NC, NT])
        tile_val = sb("tile_val", [P, NC, NT], f16)
        token_of = sb("token_of", [P, NT], i32)
        first = sb("first", [P, E + 1])
        first_i, last_i = sb("first_i", [P, E + 1], i32), sb("last_i", [P, E + 1], i32)
        first_tile, end_tile = sb("first_tile", [P, E + 1], i32), sb("end_tile", [P, E + 1], i32)
        touched = sb("touched", [P, E])
        items_of = sb("items_of", [P, E])
        item_from = sb("item_from", [P, E])
        shift = sb("shift", [P, E])
        shift_step = sb("shift_step", [P, E - 1])
        at_least_e = sb("at_least_e", [P, E - 1, NIP])
        shift_at = sb("shift_at", [P, E - 1, NIP])
        item_expert_f = sb("item_expert_f", [P, NIP])
        item_expert = sb("item_expert", [P, NIP], i32)
        item_shift = sb("item_shift", [P, NIP])
        item_tile_f = sb("item_tile_f", [P, NIP])
        past_end = sb("past_end", [P, NIP])
        item_tile = sb("item_tile", [P, NIP], i32)
        item_row = sb("item_row", [P, NIP])
        row_at_least = sb("row_at_least", [P, E, NIP])
        row_expert = sb("row_expert", [P, NIP])
        in_item = sb("in_item", [P, NIP])
        xs = sb("xs", [P, NT * D])
        bn1, bn2 = sb("bn1", [P, 6]), sb("bn2", [P, 6])
        mv1, mv2 = sb("mv1", [P, 2]), sb("mv2", [P, 2])
        var1, var2 = sb("var1", [P, 1]), sb("var2", [P, 1])
        rs1, rs2 = sb("rs1", [P, 1]), sb("rs2", [P, 1])
        rs1_in = sb("rs1_in", [P, 1])
        nm1, nm2 = sb("nm1", [P, 1]), sb("nm2", [P, 1])
        h, h2 = sb("h", [P, D]), sb("h2", [P, D])
        hT_hi, hT_lo = sb("hT_hi", [P, D], f32r), sb("hT_lo", [P, D], f32r)
        silu, gu = sb("silu", [P, D]), sb("gu", [P, D])
        gT_hi, gT_lo = sb("gT_hi", [P, D], f32r), sb("gT_lo", [P, D], f32r)
        h2T_hi, h2T_lo = sb("h2T_hi", [P, D], f32r), sb("h2T_lo", [P, D], f32r)
        scaled = sb("scaled", [P, D])
        out_rows = [sb("out_rows0", [P, D]), sb("out_rows1", [P, D])]
        out_idx = [sb("out_idx0", [P, 1], i32), sb("out_idx1", [P, 1], i32)]

        s_bn1, s_stats1 = sem("s_bn1"), sem("s_stats1")
        s_var1, s_rs1, s_rs1_in = sem("s_var1"), sem("s_rs1"), sem("s_rs1_in")
        s_const1, s_h = sem("s_const1"), sem("s_h")
        s_hT_ps, s_hT_hi, s_hT_lo = sem("s_hT_ps"), sem("s_hT_hi"), sem("s_hT_lo")
        s_z, s_silu, s_gu = sem("s_z"), sem("s_silu"), sem("s_gu")
        s_gT_ps, s_gT_hi, s_gT_lo = sem("s_gT_ps"), sem("s_gT_hi"), sem("s_gT_lo")
        s_y, s_x1 = sem("s_y"), sem("s_x1")
        s_bn2, s_stats2 = sem("s_bn2"), sem("s_stats2")
        s_var2, s_rs2 = sem("s_var2"), sem("s_rs2")
        s_const2, s_h2 = sem("s_const2"), sem("s_h2")
        s_h2T_ps, s_h2T_hi, s_h2T_lo = sem("s_h2T_ps"), sem("s_h2T_hi"), sem("s_h2T_lo")
        s_m, s_scaled, s_out, s_out_idx = sem("s_m"), sem("s_scaled"), sem("s_out"), sem("s_out_idx")
        s_xb, s_xb_last, s_out_last = sem("s_xb"), sem("s_xb_last"), sem("s_out_last")
        s_scattered = [sem("s_scattered0"), sem("s_scattered1")]
        EARLY = LOOP_FROM + 3
        s_rows = [sem(f"s_rows{j}") for j in range(EARLY)]
        s_rows_rest = sem("s_rows_rest")
        s_tid, s_bias = sem("s_tid"), sem("s_bias")
        s_nat = [sem(f"s_nat{w}") for w in range(E + 1)]
        s_ident, s_filled, s_masks, s_iotas = sem("s_ident"), sem("s_filled"), sem("s_masks"), sem("s_iotas")
        s_prep_ps, s_prep_hi, s_prep_lo = sem("s_prep_ps"), sem("s_prep_hi"), sem("s_prep_lo")
        s_row_abs, s_alpha_dram, s_alpha = sem("s_row_abs"), sem("s_alpha_dram"), sem("s_alpha")
        s_sign16, s_sign_ps, s_sign = sem("s_sign16"), sem("s_sign_ps"), sem("s_sign")
        s_lane_off, s_lane_hot, s_table = sem("s_lane_off"), sem("s_lane_hot"), sem("s_table")
        s_waited = sem("s_waited")
        s_route = sem("s_route")
        s_chunk_ps, s_rank_ps, s_slot_ps = sem("s_chunk_ps"), sem("s_rank_ps"), sem("s_slot_ps")
        s_token_of, s_item_tile = sem("s_token_of"), sem("s_item_tile")
        s_item_expert, s_in_item = sem("s_item_expert"), sem("s_in_item")

        R = {name: n + 1 for n, name in enumerate((
            "ones", "reached0", "reached_end", "reached1", "reached2", "reached3", "onehot", "chunk_sum",
            "rank", "first_i", "slot", "last_i", "lane_i", "tile_i", "first", "lane", "tile", "first_tile",
            "end_tile", "tile_hot", "lane_hot", "tile_val", "touched", "items_of", "from0", "from1", "from2", "from3",
            "shift", "shift_step", "at_least", "item_expert_f", "shift_at", "item_shift", "item_tile_f",
            "past_end", "item_row", "row_at_least", "row_expert"))}

        WEIGHT = E
        PREPS = {0: 2, 1: 3}
        SIGNS = 3
        FIRST_HALF, SECOND_HALF = range(KD // 2), range(KD // 2, KD)
        COL_HALVES = (slice(0, D // 2), slice(D // 2, D))
        prep_order = [(w, k) for w in (0, 1, *PREPS.values()) for k in range(KD)]
        prep_no = {wk: n for n, wk in enumerate(prep_order)}
        sign_banks = [*ps_prep, ps_m, ps_h2T]
        prep_banks = [*ps_prep, ps_z, ps_gT, ps_y, ps_m, ps_h2T, ps_prep[0]] + 2 * [*ps_prep, ps_m, ps_h2T]

        def prep_out(n, bank):
            return max((m + 1 for m in range(n) if prep_banks[m] is bank), default=0)

        def tile_of(buf, j):
            return buf[:, bass.ds(j * D, D)]

        def fixed(i):
            return isinstance(i, int)

        def has(j, n):
            return not fixed(j) or 0 <= j < n

        def at_least(eng, s, n):
            if not fixed(n) or n > 0:
                eng.wait_ge(s, n)

        def waited(eng):
            eng.sem_inc(s_waited, 1)

        def load(eng, table, j, top):
            return eng.value_load(table[0:1, bass.ds(j, 1)], min_val=0, max_val=top)

        def iterate(eng, body):
            for i in range(0, LOOP_FROM):
                body(i)
            with eng.Fori(LOOP_FROM, LOOP_TO) as i:
                body(i)
            for i in range(LOOP_TO, LAST_ITEM):
                body(i)

        block = ctx.enter_context(nc.Block())

        @block.sync
        def _(sp):
            sp.dma_start(tid[:], token_ids.rearrange("(p c) -> p c", p=P)).then_inc(s_tid, 16)
            for w in (0, 1, 2, 3, WEIGHT):
                if w in (2, 3):
                    sp.wait_ge(s_rows[w - 2], 16)
                src = weight if w == WEIGHT else ctx_w[w]
                sp.dma_start(nat[:, w], src.rearrange("(b p) d -> p b d", p=P)).then_inc(s_nat[w], 16)
            sp.dma_start(bias_bc[:], bias.partition_broadcast(P)).then_inc(s_bias, 16)
            sp.wait_ge(s_row_abs, KD)
            with nc.allow_non_contiguous_dma(reason="2 KB, once"):
                sp.dma_start(alpha_dram.rearrange("(b p) -> p b", p=P), row_abs[:]).then_inc(s_alpha_dram, 16)
            sp.wait_ge(s_alpha_dram, 16)
            sp.dma_start(alpha2[:], alpha_dram.partition_broadcast(P)).then_inc(s_alpha, 16)

        @block.gpsimd
        def _(pool):
            g = nc.gpsimd
            g.memset(before[:], 1.0).then_inc(s_filled, 1)
            g.memset(expert_before[:], 1.0).then_inc(s_filled, 1)
            g.memset(ident[:], 0.0).then_inc(s_filled, 1)
            g.memset(ones_col[:], 1.0).then_inc(s_masks, 1)
            g.memset(minus_half[:], -0.5).then_inc(s_masks, 1)
            pool.wait_ge(s_filled, 3)
            g.affine_select(out=before[:], in_=before[:], compare_op=ALU.is_gt, fill=0.0, base=0,
                            pattern=[[1, P]], channel_multiplier=-1).then_inc(s_masks, 1)
            g.affine_select(out=expert_before[:], in_=expert_before[:], compare_op=ALU.is_gt, fill=0.0, base=0,
                            pattern=[[NC, E + 1]], channel_multiplier=-1).then_inc(s_masks, 1)
            g.affine_select(out=ident[:], in_=ident[:], compare_op=ALU.not_equal, fill=1.0, base=0,
                            pattern=[[-1, P]], channel_multiplier=1).then_inc(s_ident, 1)
            for table, pattern, by_lane in ((iota_lane, [[1, P]], 0), (iota_item, [[1, NIP]], 0),
                                            (token_no, [[1, NC]], NC), (lane_no, [[1, 1]], 1)):
                g.iota(table[:], pattern=pattern, base=0, channel_multiplier=by_lane,
                       allow_small_or_imprecise_dtypes=True).then_inc(s_iotas, 1)

            def gather(j):
                pool.indirect_dma_start(
                    out=xs[:, j * D:(j + 1) * D], out_offset=None, in_=x,
                    in_offset=bass.IndirectOffsetOnAxis(ap=token_of[:, j:j + 1], axis=0))\
                    .then_inc(s_rows[j] if j < EARLY else s_rows_rest, 16)

            def power(j, mv, var, rs, s_stats, s_var, s_rs, s_used):
                at_least(pool, s_stats, j + 1)
                waited(pool)
                g.tensor_scalar(var[:], mv[:, 1:2], EPS, None, ALU.add).then_inc(s_var, 1)
                pool.wait_ge(s_var, j + 1)
                at_least(pool, s_used, j)
                g.tensor_tensor(rs[:], var[:], minus_half[:], ALU.pow).then_inc(s_rs, 1)
                pool.wait_ge(s_rs, j + 1)
                waited(pool)

            def constants1(j):
                power(j, mv1, var1, rs1, s_stats1, s_var1, s_rs1, s_h)
                g.tensor_tensor(rs1_in[:], rs1[:], in_item[:, bass.ds(j, 1)], ALU.mult).then_inc(s_rs1_in, 1)
                pool.wait_ge(s_rs1_in, j + 1)
                waited(pool)
                g.tensor_scalar(nm1[:], mv1[:, 0:1], rs1_in[:], -1.0, ALU.mult, ALU.mult).then_inc(s_const1, 1)

            def constants2(j):
                power(j, mv2, var2, rs2, s_stats2, s_var2, s_rs2, s_h2)
                g.tensor_scalar(nm2[:], mv2[:, 0:1], rs2[:], -1.0, ALU.mult, ALU.mult).then_inc(s_const2, 1)

            def add_bias(j):
                if fixed(j) and j == 0:
                    pool.wait_ge(s_bias, 16)
                at_least(pool, s_h2, j + 1)
                waited(pool)
                g.tensor_tensor(tile_of(xs, j), tile_of(xs, j), bias_bc[:], ALU.add).then_inc(s_xb, 1)

            def finish(j, half):
                if not fixed(j) or j >= 2:
                    pool.wait_ge(s_scattered[half], (j - half) * 8)
                g.tensor_copy(out_idx[half][:], token_of[:, bass.ds(j, 1)]).then_inc(s_out_idx, 1)
                at_least(pool, s_scaled, j + 1)
                at_least(pool, s_xb, j + 1)
                g.tensor_tensor(out_rows[half][:], tile_of(xs, j), scaled[:], ALU.add).then_inc(s_out, 1)
                pool.wait_ge(s_out, j + 1)
                pool.wait_ge(s_out_idx, j + 1)
                waited(pool)
                scatter(out_rows[half], out_idx[half][:], half)

            def scatter(rows, places, half):
                pool.indirect_dma_start(
                    out=out, out_offset=bass.IndirectOffsetOnAxis(ap=places, axis=0),
                    in_=rows[:], in_offset=None).then_inc(s_scattered[half], 16)

            pool.wait_ge(s_iotas, 4)
            pool.wait_ge(s_route, R["lane"])
            for c in range(DVE_CHUNKS, DVE_CHUNKS + POOL_CHUNKS):
                last = g.tensor_scalar(lane_hot[:, c], iota_lane[:], lane[:, c:c + 1], None, ALU.is_equal)
            last.then_inc(s_lane_hot, 1)
            pool.wait_ge(s_token_of, 1)
            for j in range(3):
                gather(j)
            pool.wait_ge(s_in_item, 1)
            constants1(0)
            gather(3)
            constants1(1)
            gather(4)
            gather(5)

            def body(i, half):
                if has(i + 2, NI):
                    constants1(i + 2)
                if has(i - LAG - 1, NT):
                    finish(i - LAG - 1, half)
                if fixed(i):
                    for j in range(6 + i * 4, min(NT, 10 + i * 4)):
                        gather(j)
                if has(i - LAG + 1, NT):
                    constants2(i - LAG + 1)
                    add_bias(i - LAG + 1)

            for i in range(0, LOOP_FROM):
                body(i, i % 2)
            with pool.Fori(LOOP_FROM, LOOP_TO, 2) as i:
                body(i, 0)
                body(i + 1, 1)
            for i in range(LOOP_TO, LAST_ITEM):
                body(i, i % 2)
            finish(LAST_TILE - 3, 0)
            constants2(LAST_TILE - 1)
            constants2(LAST_TILE)
            finish(LAST_TILE - 2, 1)
            for n, (rows, half) in enumerate(((silu, 0), (h, 1))):
                j = LAST_TILE - 1 + n
                pool.wait_ge(s_out_last, 1 + 2 * n)
                waited(pool)
                scatter(rows, token_of[:, j:j + 1], half)
            for half in range(2):
                pool.wait_ge(s_scattered[half], 16 * (NT // 2))

        @block.scalar
        def _(act):
            a = nc.scalar

            def prep_hi(w, blocks=range(KD)):
                for k in blocks:
                    n = prep_no[w, k]
                    act.wait_ge(s_prep_ps, n + 1)
                    at = (w * KD + k) * D
                    a.activation(ct_hi[:, at:at + D], prep_banks[n][:], ACT.Copy).then_inc(s_prep_hi, 1)

            def norm1(j):
                tile = load(act, item_tile, j, NT - 1)
                at_least(act, s_const1, j + 1)
                at_least(act, s_hT_ps, j)
                a.activation(h[:], tile_of(xs, tile), ACT.Identity, bias=nm1[:], scale=rs1_in[:]).then_inc(s_h, 1)

            def make_silu(i):
                if fixed(i) and i == 0:
                    act.wait_ge(s_table, 1)
                at_least(act, s_z, i + 1)
                a.activation(silu[:], ps_z[:], ACT.Silu).then_inc(s_silu, 1)

            def make_gT_hi(i, hi):
                at_least(act, s_gT_ps, i + 1)
                a.activation(hi[:], ps_gT[:], ACT.Copy).then_inc(s_gT_hi, 1)

            def make_h2T_hi(j):
                at_least(act, s_h2T_ps, j + 1)
                at_least(act, s_m, j)
                a.activation(h2T_hi[:], ps_h2T[:], ACT.Copy).then_inc(s_h2T_hi, 1)

            def norm2(j):
                at_least(act, s_const2, j + 1)
                at_least(act, s_h2T_ps, j)
                a.activation(h2[:], tile_of(xs, j), ACT.Identity, bias=nm2[:], scale=rs2[:]).then_inc(s_h2, 1)

            def body(i):
                if has(i, NI):
                    make_silu(i)
                if has(i + 1, NI):
                    at_least(act, s_hT_ps, i + 2)
                    a.activation(hT_hi[:], ps_hT[:], ACT.Copy).then_inc(s_hT_hi, 1)
                if has(i - LAG, NT):
                    make_h2T_hi(i - LAG)
                if fixed(i) and i in PREPS:
                    prep_hi(PREPS[i])
                if fixed(i) and i == SIGNS:
                    for k in range(KD):
                        act.wait_ge(s_sign_ps, k + 1)
                        a.activation(half_sign[:, k], sign_banks[k][:].bitcast(f16)[:, 0:D], ACT.Copy)\
                         .then_inc(s_sign, 1)
                if has(i + 2, NI):
                    norm1(i + 2)
                if has(i, NI):
                    make_gT_hi(i, gT_hi)
                if has(i - LAG + 1, NT) and not (fixed(i) and i == LAST_ITEM - 1):
                    norm2(i - LAG + 1)
                if fixed(i) and i in (1, 2):
                    act.wait_ge(s_nat[WEIGHT], 16)
                    for b in (FIRST_HALF, SECOND_HALF)[i - 1]:
                        a.activation(silu[:], nat[:, WEIGHT, b], ACT.Abs, scale=2.0 / D,
                                     accum_out=row_abs[:, b:b + 1]).then_inc(s_row_abs, 1)
                        act.wait_ge(s_row_abs, b + 1)

            act.wait_ge(s_route, R["ones"])
            a.activation(silu[:, 0:1], ones[:, 0:1], ACT.Silu).then_inc(s_table, 1)
            act.wait_ge(s_iotas, 1)
            act.wait_ge(s_route, R["lane"])
            for c in range(ACT_CHUNKS):
                a.activation(lane_off[:, c], iota_lane[:], ACT.Abs, bias=lane[:, NC - ACT_CHUNKS + c:][:, 0:1],
                             scale=-1.0).then_inc(s_lane_off, 1)
            act.wait_ge(s_lane_off, ACT_CHUNKS)
            a.activation(lane_hot[:, NC - ACT_CHUNKS:], lane_off[:], ACT.Relu, bias=ones[:, 0:1],
                         scale=-1.0).then_inc(s_lane_hot, 1)
            prep_hi(0)
            prep_hi(1)
            act.wait_ge(s_item_tile, 1)
            norm1(0)
            act.wait_ge(s_hT_ps, 1)
            a.activation(hT_hi[:], ps_hT[:], ACT.Copy).then_inc(s_hT_hi, 1)
            norm1(1)
            iterate(act, body)
            make_silu(LAST_ITEM)
            norm2(LAST_TILE - 2)
            make_gT_hi(LAST_ITEM, hT_hi)
            make_h2T_hi(LAST_TILE - 2)
            norm2(LAST_TILE - 1)
            make_h2T_hi(LAST_TILE - 1)
            norm2(LAST_TILE)
            act.wait_ge(s_h2T_ps, NT)
            act.wait_ge(s_y, LAST_ITEM)
            a.activation(gT_hi[:], ps_h2T[:], ACT.Copy).then_inc(s_h2T_hi, 1)

        @block.vector
        def _(dve):
            v = nc.vector

            def step(name, ins):
                ins.then_inc(s_route, 1)

            def after(name):
                dve.wait_ge(s_route, R[name])

            def by_item(ap, n):
                return ap.unsqueeze(1).broadcast_to([P, n, NIP])

            def by_expert(ap, n):
                return ap.unsqueeze(2).broadcast_to([P, n, NIP])

            def over_experts(ap):
                return ap.rearrange("p e t -> p t e")

            step("ones", v.memset(ones[:], 1.0))
            step("reached0", v.memset(reached[:, 0], 1.0))
            step("reached_end", v.memset(reached[:, E], 0.0))
            dve.wait_ge(s_tid, 16)
            for e in range(1, E):
                step(f"reached{e}", v.tensor_scalar(reached[:, e], tid[:], float(PER_EXPERT * e), None, ALU.is_ge))
            v.memset(onehot[:, E:2 * E], 0.0).then_inc(s_masks, 1)
            after("reached3")
            step("onehot", v.tensor_tensor(onehot[:, 0:E], reached[:, 0:E], reached[:, 1:E + 1], ALU.subtract))
            dve.wait_ge(s_chunk_ps, 1)
            step("chunk_sum", v.tensor_scalar(chunk_sum[:], ones[:], ps_chunk_sum, None, ALU.mult))
            dve.wait_ge(s_rank_ps, 1)
            step("rank", v.tensor_tensor(rank[:], ps_rank.rearrange("p (e c) -> p e c", e=E), onehot[:, 0:E],
                                         ALU.mult))
            step("first_i", v.tensor_copy(first_i[:], ps_first))
            after("rank")
            with nc.allow_low_precision(reason="whole numbers below 2^12"):
                step("slot", v.tensor_reduce(slot[:], rank[:].rearrange("p e c -> p c e"), AX.X, ALU.add))
            step("last_i", v.tensor_scalar(last_i[:], ps_first, float(P - 1), None, ALU.add))
            after("slot")
            step("lane_i", v.tensor_scalar(lane_i[:], slot[:], P - 1, None, ALU.bitwise_and))
            step("tile_i", v.tensor_scalar(tile_i[:], slot[:], LOG_P, None, ALU.logical_shift_right))
            step("first", v.tensor_copy(first[:], ps_first))
            after("tile_i")
            step("lane", v.tensor_copy(lane[:], lane_i[:]))
            step("tile", v.tensor_copy(tile[:], tile_i[:]))
            step("first_tile", v.tensor_scalar(first_tile[:], first_i[:], LOG_P, None, ALU.logical_shift_right))
            step("end_tile", v.tensor_scalar(end_tile[:], last_i[:], LOG_P, None, ALU.logical_shift_right))
            dve.wait_ge(s_iotas, 4)
            after("tile")
            step("tile_hot", v.tensor_tensor(tile_hot[:], tile[:].unsqueeze(2).broadcast_to([P, NC, NT]),
                                             iota_item[:, 0:NT].unsqueeze(1).broadcast_to([P, NC, NT]), ALU.is_equal))
            for c in range(DVE_CHUNKS):
                last = v.tensor_scalar(lane_hot[:, c], iota_lane[:], lane[:, c:c + 1], None, ALU.is_equal)
            step("lane_hot", last)
            after("tile_hot")
            step("tile_val", v.tensor_tensor(tile_val[:], tile_hot[:],
                                             token_no[:].unsqueeze(2).broadcast_to([P, NC, NT]), ALU.mult))
            after("end_tile")
            step("touched", v.tensor_tensor(touched[:], end_tile[:, 1:E + 1], first_tile[:, 0:E], ALU.subtract))
            after("touched")
            step("items_of", v.tensor_scalar(items_of[:], touched[:], 1.0, None, ALU.max))
            step("from0", v.memset(item_from[:, 0:1], 0.0))
            for e in range(1, E):
                after(f"from{e - 1}")
                step(f"from{e}", v.tensor_tensor(item_from[:, e:e + 1], item_from[:, e - 1:e],
                                                 items_of[:, e - 1:e], ALU.add))
            dve.wait_ge(s_slot_ps, 1)
            v.tensor_copy(token_of[:], ps_slot).then_inc(s_token_of, 1)
            after("from3")
            step("shift", v.tensor_tensor(shift[:], first_tile[:, 0:E], item_from[:], ALU.subtract))
            after("shift")
            step("shift_step", v.tensor_tensor(shift_step[:], shift[:, 1:E], shift[:, 0:E - 1], ALU.subtract))
            step("at_least", v.tensor_tensor(at_least_e[:], by_item(iota_item[:], E - 1),
                                             by_expert(item_from[:, 1:E], E - 1), ALU.is_ge))
            after("at_least")
            step("item_expert_f", v.tensor_reduce(item_expert_f[:], over_experts(at_least_e[:]), AX.X, ALU.add))
            step("shift_at", v.tensor_tensor(shift_at[:], at_least_e[:], by_expert(shift_step[:], E - 1), ALU.mult))
            after("shift_at")
            step("item_shift", v.tensor_reduce(item_shift[:], over_experts(shift_at[:]), AX.X, ALU.add))
            v.tensor_copy(item_expert[:], item_expert_f[:]).then_inc(s_item_expert, 1)
            after("item_shift")
            step("item_tile_f", v.tensor_tensor(item_tile_f[:], item_shift[:], iota_item[:], ALU.add))
            after("item_tile_f")
            step("past_end", v.tensor_scalar(past_end[:], item_tile_f[:], float(NT), -float(NT), ALU.is_ge, ALU.mult))
            step("item_row", v.tensor_scalar(item_row[:], item_tile_f[:], float(P), lane_no[:], ALU.mult, ALU.add))
            after("past_end")
            v.tensor_tensor(item_tile[:], item_tile_f[:], past_end[:], ALU.add).then_inc(s_item_tile, 1)
            after("item_row")
            step("row_at_least", v.tensor_tensor(row_at_least[:], by_item(item_row[:], E),
                                                 by_expert(first[:, 1:E + 1], E), ALU.is_ge))
            after("row_at_least")
            step("row_expert", v.tensor_reduce(row_expert[:], over_experts(row_at_least[:]), AX.X, ALU.add))
            after("row_expert")
            v.tensor_tensor(in_item[:], row_expert[:], item_expert_f[:], ALU.is_equal).then_inc(s_in_item, 1)

            def prep_lo(w, blocks=range(KD)):
                for k in blocks:
                    n = prep_no[w, k]
                    dve.wait_ge(s_prep_hi, n + 1)
                    at = (w * KD + k) * D
                    v.tensor_tensor(ct_lo[:, at:at + D], prep_banks[n][:], ct_hi[:, at:at + D].bitcast(f32),
                                    ALU.subtract).then_inc(s_prep_lo, 1)

            def stats1(j, tile):
                if fixed(j) and j < EARLY:
                    dve.wait_ge(s_rows[j], 16)
                at_least(dve, s_stats1, j)
                waited(dve)
                v.bn_stats(bn1[:], tile_of(xs, tile)).then_inc(s_bn1, 1)
                dve.wait_ge(s_bn1, j + 1)
                at_least(dve, s_const1, j)
                waited(dve)
                v.bn_aggr(mv1[:], bn1[:]).then_inc(s_stats1, 1)

            def rest(lo, ps, hi, s_hi, s_lo, j):
                at_least(dve, s_hi, j + 1)
                v.tensor_tensor(lo[:], ps[:], hi[:].bitcast(f32), ALU.subtract).then_inc(s_lo, 1)

            def residual(j, tile, ps=ps_y):
                at_least(dve, s_h, min(j + E, NI) if fixed(j) else j + E)
                at_least(dve, s_x1, j)
                at_least(dve, s_y, j + 1)
                v.tensor_tensor(tile_of(xs, tile), ps[:], tile_of(xs, tile), ALU.add).then_inc(s_x1, 1)

            def stats2(j):
                dve.wait_ge(s_x1, j + E)
                at_least(dve, s_stats2, j)
                waited(dve)
                v.bn_stats(bn2[:], tile_of(xs, j)).then_inc(s_bn2, 1)
                dve.wait_ge(s_bn2, j + 1)
                at_least(dve, s_const2, j)
                waited(dve)
                v.bn_aggr(mv2[:], bn2[:]).then_inc(s_stats2, 1)

            def scale(j):
                if fixed(j) and j == 0:
                    dve.wait_ge(s_alpha, 16)
                at_least(dve, s_m, j + 1)
                at_least(dve, s_out, j)
                v.tensor_tensor(scaled[:], ps_m[:], alpha2[:], ALU.mult).then_inc(s_scaled, 1)

            def gate(i):
                at_least(dve, s_silu, i + 1)
                at_least(dve, s_gT_ps, i)
                v.tensor_tensor(gu[:], ps_z[:], silu[:], ALU.mult).then_inc(s_gu, 1)

            def add_bias(j):
                dve.wait_ge(s_bias, 16)
                dve.wait_ge(s_h2, j + 1)
                v.tensor_tensor(tile_of(xs, j), tile_of(xs, j), bias_bc[:], ALU.add).then_inc(s_xb_last, 1)

            def body(i):
                next_tile = load(dve, item_tile, i + 3, NT - 1) if has(i + 3, NI) else None
                prev_tile = load(dve, item_tile, i - 1, NT - 1) if has(i - 1, NI) else None
                if has(i - LAG - 1, NT):
                    scale(i - LAG - 1)
                if has(i, NI):
                    gate(i)
                if has(i + 1, NI):
                    rest(hT_lo, ps_hT, hT_hi, s_hT_hi, s_hT_lo, i + 1)
                if has(i - LAG, NT):
                    rest(h2T_lo, ps_h2T, h2T_hi, s_h2T_hi, s_h2T_lo, i - LAG)
                if fixed(i) and i in PREPS:
                    prep_lo(PREPS[i])
                if fixed(i) and i == SIGNS - 1:
                    dve.wait_ge(s_nat[WEIGHT], 16)
                    for b in range(KD):
                        v.tensor_scalar(sign16[:, b], nat[:, WEIGHT, b], 0.0, -0.5, ALU.is_ge, ALU.add)\
                         .then_inc(s_sign16, 1)
                    dve.wait_ge(s_ident, 1)
                    v.tensor_copy(ident16[:], ident[:]).then_inc(s_sign16, 1)
                if has(i + 3, NI):
                    stats1(i + 3, next_tile)
                if has(i - 1, NI):
                    residual(i - 1, prev_tile)
                if has(i - LAG + 1, NT):
                    stats2(i - LAG + 1)
                if has(i, NI):
                    rest(gT_lo, ps_gT, gT_hi, s_gT_hi, s_gT_lo, i)
                if fixed(i) and i == LOOP_FROM - 1:
                    dve.wait_ge(s_rows_rest, 16 * (NT - EARLY))

            prep_lo(0, range(1))
            stats1(0, 0)
            prep_lo(0, range(1, KD))
            dve.wait_ge(s_item_tile, 1)
            stats1(1, load(dve, item_tile, 1, NT - 1))
            rest(hT_lo, ps_hT, hT_hi, s_hT_hi, s_hT_lo, 0)
            prep_lo(1)
            stats1(2, load(dve, item_tile, 2, NT - 1))
            iterate(dve, body)
            tile_17, tile_18 = (load(dve, item_tile, j, NT - 1) for j in (LAST_ITEM - 1, LAST_ITEM))
            gate(LAST_ITEM)
            scale(LAST_TILE - 3)
            rest(hT_lo, ps_gT, hT_hi, s_gT_hi, s_gT_lo, LAST_ITEM)
            rest(h2T_lo, ps_h2T, h2T_hi, s_h2T_hi, s_h2T_lo, LAST_TILE - 2)
            residual(LAST_ITEM - 1, tile_17)
            stats2(LAST_TILE - 1)
            residual(LAST_ITEM, tile_18, ps_hT)
            stats2(LAST_TILE)
            scale(LAST_TILE - 2)
            rest(h2T_lo, ps_h2T, h2T_hi, s_h2T_hi, s_h2T_lo, LAST_TILE - 1)
            add_bias(LAST_TILE - 1)
            add_bias(LAST_TILE)
            rest(gT_lo, ps_h2T, gT_hi, s_h2T_hi, s_h2T_lo, LAST_TILE)
            scale(LAST_TILE - 1)
            dve.wait_ge(s_xb_last, 2)
            dve.wait_ge(s_scaled, LAST_TILE)
            v.tensor_tensor(silu[:], tile_of(xs, LAST_TILE - 1), scaled[:], ALU.add).then_inc(s_out_last, 1)
            for n, (ps, cols) in enumerate(zip((ps_z, ps_gT), COL_HALVES)):
                dve.wait_ge(s_m, NT + n)
                v.tensor_tensor(gu[:, cols], ps[:, cols], alpha2[:, cols], ALU.mult).then_inc(s_scaled, 1)
                dve.wait_ge(s_scaled, NT + n)
                v.tensor_tensor(h[:, cols], xs[:, LAST_TILE * D:][:, cols], gu[:, cols], ALU.add)\
                 .then_inc(s_out_last, 1)

        @block.tensor
        def _(pe):
            t = nc.tensor
            pe.wait_ge(s_masks, 5)
            pe.wait_ge(s_route, R["onehot"])
            flat = onehot[:].rearrange("p e c -> p (e c)")
            t.matmul(ps_chunk_sum, flat, ones_col[:, 0:1], start=True, stop=True).then_inc(s_chunk_ps, 1)
            t.matmul(ps_rank, before[:], flat[:, 0:E * NC], start=True, stop=False)
            pe.wait_ge(s_route, R["chunk_sum"])
            t.matmul(ps_rank, chunk_sum[:], before[:, 0:E * NC], start=False, stop=True)
            t.matmul(ps_first, chunk_sum[:], expert_before[:], start=True, stop=True).then_inc(s_rank_ps, 1)

            def transpose(ps, src, identity=ident):
                for b in range(KD):
                    last = t.transpose(ps[:, b * P:(b + 1) * P], src(b), identity[:])
                return last

            def prep(w, blocks=range(KD)):
                pe.wait_ge(s_nat[w], 16)
                for k in blocks:
                    n = prep_no[w, k]
                    at_least(pe, s_prep_lo, prep_out(n, prep_banks[n]))
                    transpose(prep_banks[n], lambda b: nat[:, w, b, k * P:(k + 1) * P]).then_inc(s_prep_ps, 1)

            def warm(times):
                pe.wait_ge(s_prep_hi, 1)
                pe.wait_ge(s_prep_lo, 2)
                for _ in range(times):
                    t.matmul(ps_prep[1][:], ct_hi[:, 0:P], ct_hi[:, 0:D], start=True, stop=True)

            def transpose1(j):
                at_least(pe, s_h, j + 1)
                at_least(pe, s_hT_lo, j)
                transpose(ps_hT, lambda b: h[:, b * P:(b + 1) * P]).then_inc(s_hT_ps, 1)

            def transpose2(j):
                at_least(pe, s_h2, j + 1)
                at_least(pe, s_h2T_lo, j)
                transpose(ps_h2T, lambda b: h2[:, b * P:(b + 1) * P]).then_inc(s_h2T_ps, 1)

            def product(ps, hi, lo, expert, blocks=range(KD)):
                for k in blocks:
                    blk = slice(k * P, (k + 1) * P)
                    c_hi = ct_hi[:, bass.ds(expert * (KD * D) + k * D, D)]
                    c_lo = ct_lo[:, bass.ds(expert * (KD * D) + k * D, D)]
                    t.matmul(ps[:], hi[:, blk], c_hi, start=(k == 0), stop=False)
                    t.matmul(ps[:], hi[:, blk], c_lo, start=False, stop=False)
                    last = t.matmul(ps[:], lo[:, blk], c_hi, start=False, stop=(k == KD - 1))
                return last

            def product1(i, expert):
                at_least(pe, s_hT_lo, i + 1)
                at_least(pe, s_gu, i)
                if fixed(i) and i < E:
                    pe.wait_ge(s_prep_lo, prep_no[i, KD - 1] + 1)
                product(ps_z, hT_hi, hT_lo, expert).then_inc(s_z, 1)

            def transpose_g(i):
                at_least(pe, s_gu, i + 1)
                at_least(pe, s_gT_lo, i)
                transpose(ps_gT, lambda b: gu[:, b * P:(b + 1) * P]).then_inc(s_gT_ps, 1)

            def start_product2(j):
                at_least(pe, s_gT_lo, j + 1)
                at_least(pe, s_x1, j)

            def product2(j, expert):
                start_product2(j)
                product(ps_y, gT_hi, gT_lo, expert).then_inc(s_y, 1)

            def product3(ps, hi, lo, blocks=range(KD), cols=slice(0, D)):
                for k in blocks:
                    blk = slice(k * P, (k + 1) * P)
                    sign = half_sign[:, k, cols]
                    t.matmul(ps[:, cols], hi[:, blk], sign, start=(k == 0), stop=False)
                    last = t.matmul(ps[:, cols], lo[:, blk], sign, start=False, stop=(k == KD - 1))
                return last

            def start_product3(j):
                if fixed(j) and j == 0:
                    pe.wait_ge(s_sign, KD)
                at_least(pe, s_h2T_lo, j + 1)
                at_least(pe, s_scaled, j)

            def expert_of(i):
                return e_first[i] if fixed(i) and i in e_first else load(pe, item_expert, i, E - 1)

            def body(i):
                e_now = expert_of(i)
                e_prev = expert_of(i - 1) if has(i - 1, NI) else None
                if has(i, NI):
                    product1(i, e_now)
                late = fixed(i) and i in (LAG, LAG + 1)
                if has(i + 1, NI):
                    transpose1(i + 1)
                if has(i - LAG, NT) and not late:
                    transpose2(i - LAG)
                if fixed(i) and i in PREPS:
                    prep(PREPS[i])
                if fixed(i) and i == SIGNS:
                    pe.wait_ge(s_sign16, KD + 1)
                    pe.wait_ge(s_prep_lo, len(prep_order))
                    for k in range(KD):
                        transpose(sign_banks[k][:].bitcast(f16), lambda b: sign16[:, b, k * P:(k + 1) * P], ident16)\
                            .then_inc(s_sign_ps, 1)
                if late:
                    start_product2(i - 1)
                    product(ps_y, gT_hi, gT_lo, e_prev, FIRST_HALF)
                    transpose2(i - LAG)
                    product(ps_y, gT_hi, gT_lo, e_prev, SECOND_HALF).then_inc(s_y, 1)
                elif has(i - 1, NI):
                    product2(i - 1, e_prev)
                if has(i, NI):
                    transpose_g(i)
                if has(i - LAG, NT) and not (fixed(i) and i == LAST_ITEM - 1):
                    start_product3(i - LAG)
                    product3(ps_m, h2T_hi, h2T_lo).then_inc(s_m, 1)

            pe.wait_ge(s_ident, 1)
            prep(0, range(1))
            pe.wait_ge(s_route, R["tile_val"])
            pe.wait_ge(s_lane_hot, 2)
            for c in range(NC):
                last = t.matmul(ps_slot, lane_hot[:, c], tile_val[:, c], start=(c == 0), stop=(c == NC - 1))
            last.then_inc(s_slot_ps, 1)
            prep(0, range(1, KD))
            prep(1)
            warm(8)
            transpose1(0)
            warm(7)
            pe.wait_ge(s_item_expert, 1)
            e_first = {j: load(pe, item_expert, j, E - 1) for j in (0, 1)}
            iterate(pe, body)
            e_17, e_18 = (load(pe, item_expert, j, E - 1) for j in (LAST_ITEM - 1, LAST_ITEM))
            product1(LAST_ITEM, e_18)
            start_product3(LAST_TILE - 3)
            product3(ps_m, h2T_hi, h2T_lo).then_inc(s_m, 1)
            transpose_g(LAST_ITEM)
            transpose2(LAST_TILE - 2)
            product2(LAST_ITEM - 1, e_17)
            pe.wait_ge(s_gT_lo, NI)
            product(ps_hT, hT_hi, hT_lo, e_18).then_inc(s_y, 1)
            start_product3(LAST_TILE - 2)
            product3(ps_m, h2T_hi, h2T_lo).then_inc(s_m, 1)
            transpose2(LAST_TILE - 1)
            start_product3(LAST_TILE - 1)
            product3(ps_m, h2T_hi, h2T_lo, range(1))
            transpose2(LAST_TILE)
            product3(ps_m, h2T_hi, h2T_lo, range(1, KD)).then_inc(s_m, 1)
            pe.wait_ge(s_h2T_lo, NT)
            for ps, cols in zip((ps_z, ps_gT), COL_HALVES):
                product3(ps, gT_hi, gT_lo, cols=cols).then_inc(s_m, 1)


def kernel(x, itok_BxS_13_99985, ctx_2048, L0_ffn_weight, L0_ffn_bias):
    import numpy as np
    import concourse.bacc as bacc
    from concourse.bass_utils import run_bass_kernel_spmd

    given = {"x": np.ascontiguousarray(x).reshape(T, D), "token_ids": np.ascontiguousarray(itok_BxS_13_99985).reshape(T),
             "ctx_w": np.ascontiguousarray(ctx_2048), "weight": np.ascontiguousarray(L0_ffn_weight),
             "bias": np.ascontiguousarray(L0_ffn_bias)}
    nc = bacc.Bacc("TRN2", target_bir_lowering=False, num_devices=1)
    args = [nc.dram_tensor(f"in_{n}", a.shape, mybir.dt.from_np(a.dtype), kind="ExternalInput").ap()
            for n, a in given.items()]
    out = nc.dram_tensor("out_rows_dram", (T, D), mybir.dt.float32, kind="ExternalOutput").ap()
    xattn_ffn(nc, *args, out)
    r = run_bass_kernel_spmd(nc, [{f"in_{n}": a for n, a in given.items()}], core_ids=[0])
    return r.results[0]["out_rows_dram"].reshape(4, 512, D)
```
